# Optimizing a Trainium2 kernel written in Bass

```python
import numpy as np
import jax
import jax.numpy as jnp

def _softmax(x, axis=-1):
    return jax.nn.softmax(x, axis=axis)

def _gelu(x):
    return jax.nn.gelu(x, approximate=True)

def _silu(x):
    return jax.nn.silu(x)

def _sigmoid(x):
    return jax.nn.sigmoid(x)

def _layernorm(x, axis=-1, eps=1e-05):
    m = jnp.mean(x, axis=axis, keepdims=True)
    v = jnp.var(x, axis=axis, keepdims=True)
    return (x - m) / jnp.sqrt(v + eps)

def _scatter_add(tgt, idx, src, axis=0):
    return tgt.at[idx].add(src)

def _segment_sum(src, seg, n):
    return jax.ops.segment_sum(src, seg, n)
kernel_name = 'mk_gnn_preln_d2_gnn_r8_84fc8e'

def setup_inputs(seed: int=0):
    np.random.seed(seed)
    _w = jnp.asarray

    def _rec_inputs():
        import jax
        import jax.numpy as jnp
        _gk = jax.random.key(seed)
        x = -0.000202 + 1 * jax.random.normal(jax.random.fold_in(_gk, 1), (6250, 128), jnp.float32)
        src = jax.random.randint(jax.random.fold_in(_gk, 2), (200000,), 0, 6250, jnp.int32)
        dst = jax.random.randint(jax.random.fold_in(_gk, 3), (200000,), 0, 6250, jnp.int32)
        _o = jnp.argsort(dst, stable=True)
        src = src[_o]
        dst = dst[_o]
        edge_attr_128 = -5.16925e-05 + 1.00005 * jax.random.normal(jax.random.fold_in(_gk, 11), (200000, 128), jnp.float32)
        return (x, src, dst, edge_attr_128)
    x, src, dst, edge_attr_128 = _rec_inputs()

    def _L0_gnn_setup():
        import jax, jax.numpy as jnp
        import numpy as np
        N, E, D = (6250, 100000, 128)
        LN_EPS = 1e-05
        key = jax.random.key(seed)
        ks = jax.random.split(key, 8)
        x = jax.random.normal(ks[0], (N, D), dtype=jnp.float32)
        edge_index = jax.random.randint(ks[1], (2, E), 0, N, dtype=jnp.int64)
        edge_attr = jax.random.normal(ks[2], (E, D), dtype=jnp.float32)
        s_msg = 1.0 / np.sqrt(2 * D)
        s_upd = 1.0 / np.sqrt(2 * D)
        W_msg = jax.random.uniform(ks[3], (2 * D, D), jnp.float32, -s_msg, s_msg)
        b_msg = jax.random.uniform(ks[4], (D,), jnp.float32, -s_msg, s_msg)
        W_upd = jax.random.uniform(ks[5], (2 * D, D), jnp.float32, -s_upd, s_upd)
        b_upd = jax.random.uniform(ks[6], (D,), jnp.float32, -s_upd, s_upd)
        gamma = jnp.ones((D,), jnp.float32)
        beta = jnp.zeros((D,), jnp.float32)
        return {'x': x, 'edge_index': edge_index, 'edge_attr': edge_attr, 'W_msg': W_msg, 'b_msg': b_msg, 'W_upd': W_upd, 'b_upd': b_upd, 'gamma': gamma, 'beta': beta}
    _L0_gnn_all = _L0_gnn_setup()
    _L0_gnn_in = {k: v for k, v in _L0_gnn_all.items() if k in ('W_msg', 'b_msg', 'W_upd', 'b_upd', 'gamma', 'beta')}
    del _L0_gnn_all

    def _L1_gnn_setup():
        import jax, jax.numpy as jnp
        import numpy as np
        N_NODES = 12500
        N_EDGES = 200000
        F_IN = 128
        F_HID = 16

        def _gcn_conv(x, src, dst, W, b, n):
            h = x @ W
            deg = jax.ops.segment_sum(jnp.ones_like(dst, dtype=h.dtype), dst, num_segments=n)
            dinv = jnp.where(deg > 0, jax.lax.rsqrt(deg), 0.0)
            norm = dinv[src] * dinv[dst]
            msg = h[src] * norm[:, None]
            out = jax.ops.segment_sum(msg, dst, num_segments=n)
            return out + b
        key = jax.random.key(seed)
        k1, k2, k3, k4 = jax.random.split(key, 4)
        x = jax.random.normal(k1, (N_NODES, F_IN), dtype=jnp.float32)
        edge_index = jax.random.randint(k2, (2, N_EDGES), 0, N_NODES, dtype=jnp.int64)
        W1 = jax.random.normal(k3, (F_IN, F_HID), dtype=jnp.float32) * (1.0 / np.sqrt(F_IN))
        b1 = jnp.zeros((F_HID,), dtype=jnp.float32)
        W2 = jax.random.normal(k4, (F_HID, F_IN), dtype=jnp.float32) * (1.0 / np.sqrt(F_HID))
        b2 = jnp.zeros((F_IN,), dtype=jnp.float32)
        return {'x': x, 'edge_index': edge_index, 'W1': W1, 'b1': b1, 'W2': W2, 'b2': b2}
    _L1_gnn_all = _L1_gnn_setup()
    _L1_gnn_in = {k: v for k, v in _L1_gnn_all.items() if k in ('W1', 'b1', 'W2', 'b2')}
    del _L1_gnn_all
    return {'x': x, 'src': src, 'dst': dst, 'edge_attr_128': edge_attr_128, 'L0_gnn_W_msg': _L0_gnn_in['W_msg'], 'L0_gnn_b_msg': _L0_gnn_in['b_msg'], 'L0_gnn_W_upd': _L0_gnn_in['W_upd'], 'L0_gnn_b_upd': _L0_gnn_in['b_upd'], 'L0_gnn_gamma': _L0_gnn_in['gamma'], 'L0_gnn_beta': _L0_gnn_in['beta'], 'L1_gnn_W1': _L1_gnn_in['W1'], 'L1_gnn_b1': _L1_gnn_in['b1'], 'L1_gnn_W2': _L1_gnn_in['W2'], 'L1_gnn_b2': _L1_gnn_in['b2']}

def reference(x, src, dst, edge_attr_128, L0_gnn_W_msg, L0_gnn_b_msg, L0_gnn_W_upd, L0_gnn_b_upd, L0_gnn_gamma, L0_gnn_beta, L1_gnn_W1, L1_gnn_b1, L1_gnn_W2, L1_gnn_b2):
    import jax
    import jax.numpy as jnp

    def _L0_gnn_ref(x, edge_index, edge_attr, W_msg, b_msg, W_upd, b_upd, gamma, beta):
        import jax, jax.numpy as jnp
        import numpy as np
        N, E, D = (6250, 100000, 128)
        LN_EPS = 1e-05
        src, dst = (edge_index[0], edge_index[1])
        n = x.shape[0]
        msg_in = jnp.concatenate([x[src], edge_attr], axis=-1)
        msg = jax.nn.relu(msg_in @ W_msg + b_msg)
        summed = jax.ops.segment_sum(msg, dst, num_segments=n)
        counts = jax.ops.segment_sum(jnp.ones((msg.shape[0],), x.dtype), dst, num_segments=n)
        mean_msg = summed / jnp.maximum(counts, 1.0)[:, None]
        h = jnp.concatenate([x, mean_msg], axis=-1) @ W_upd + b_upd
        mu = jnp.mean(h, axis=-1, keepdims=True)
        var = jnp.mean(jnp.square(h - mu), axis=-1, keepdims=True)
        h = (h - mu) * jax.lax.rsqrt(var + LN_EPS) * gamma + beta
        return jax.nn.relu(h + x)

    def _L1_gnn_ref(x, edge_index, W1, b1, W2, b2):
        import jax, jax.numpy as jnp
        import numpy as np
        N_NODES = 12500
        N_EDGES = 200000
        F_IN = 128
        F_HID = 16

        def _gcn_conv(x, src, dst, W, b, n):
            h = x @ W
            deg = jax.ops.segment_sum(jnp.ones_like(dst, dtype=h.dtype), dst, num_segments=n)
            dinv = jnp.where(deg > 0, jax.lax.rsqrt(deg), 0.0)
            norm = dinv[src] * dinv[dst]
            msg = h[src] * norm[:, None]
            out = jax.ops.segment_sum(msg, dst, num_segments=n)
            return out + b
        n = x.shape[0]
        loop = jnp.arange(n, dtype=edge_index.dtype)
        src = jnp.concatenate([edge_index[0], loop])
        dst = jnp.concatenate([edge_index[1], loop])
        h = _gcn_conv(x, src, dst, W1, b1, n)
        h = jax.nn.relu(h)
        out = _gcn_conv(h, src, dst, W2, b2, n)
        return out
    edge_index = jnp.stack([src, dst])
    h = jnp.maximum(_layernorm(x, axis=-1), 0.0)
    x = x + _L0_gnn_ref(h, edge_index, edge_attr_128, L0_gnn_W_msg, L0_gnn_b_msg, L0_gnn_W_upd, L0_gnn_b_upd, L0_gnn_gamma, L0_gnn_beta)
    h = jnp.maximum(_layernorm(x, axis=-1), 0.0)
    x = x + _L1_gnn_ref(h, edge_index, L1_gnn_W1, L1_gnn_b1, L1_gnn_W2, L1_gnn_b2)
    return x

_drawn_inputs = setup_inputs


def setup_inputs(seed=0):
    import zlib

    import numpy as np

    out = dict(_drawn_inputs(seed))
    spreads = {'L0_gnn_gamma': (1.0, 0.2),
     'L0_gnn_beta': (0.0, 0.1),
     'L1_gnn_b1': (0.0, 0.1),
     'L1_gnn_b2': (0.0, 0.1)}
    factors = {'L0_gnn_b_msg': 5.16}
    for name, (base, spread) in spreads.items():
        noise = np.random.default_rng([zlib.crc32(name.encode()), seed]).standard_normal(out[name].shape)
        drawn = base * np.exp(spread * noise) if base else spread * noise
        out[name] = jnp.asarray(drawn.astype(out[name].dtype))
    for name, factor in factors.items():
        out[name] = (out[name] * factor).astype(out[name].dtype)
    return out
```

```python
import concourse.bass as bass
from concourse import mybir
from contextlib import ExitStack

F32 = mybir.dt.float32
I32 = mybir.dt.int32
ALU = mybir.AluOpType
ACT = mybir.ActivationFunctionType
AX = mybir.AxisListType
P = 128
EPS = 1e-5


def gnn_kernel(nc, x, src, dst, edge_attr, W_msg, b_msg, W_upd, b_upd, gamma, beta, W1, b1, W2, b2, out):
    N, D = x.shape
    E = src.shape[0]
    HID = W1.shape[1]
    NT = -(-N // P)
    FULL = N // P
    TAIL = N - FULL * P
    TILES = -(-E // N) + 2
    CHUNK = TILES * P
    GT = 512 // D
    GROUPS = [(g, min(GT, TILES - g)) for g in range(0, TILES, GT)]
    NG = len(GROUPS)
    LAST_START = E - CHUNK
    CHUNKS = -(-E // CHUNK)
    BT = 7
    NB = NT // BT
    assert NT % BT == 0 and NT % 2 == 1
    SP_ = 125
    STRIDE = 16
    PER = E // SP_
    assert PER % STRIDE == 0 and D == P

    ctx = ExitStack()
    with ctx:
        def sb(name, shape, dt=F32):
            return ctx.enter_context(nc.sbuf_tensor(name, shape, dt))

        def sem(name):
            return ctx.enter_context(nc.semaphore(name))

        used = []

        def phase_sem(name):
            s = sem(name)
            used.append(s)
            return s

        def clear(sems):
            for s in sems:
                nc.sync.sem_clear(s)
            nc.all_engine_barrier()

        y_table = nc.dram_tensor("y_table", [NT * P, D], F32)
        z1_table = nc.dram_tensor("z1_table", [NT * P, HID], F32)
        z2_table = nc.dram_tensor("z2_table", [NT * P, HID], F32)
        dst_any = nc.dram_tensor("dst_any", [CHUNKS * CHUNK], I32)

        x_sb = sb("x_sb", [P, NT, D])
        h_sb = sb("h_sb", [P, NT, D])
        agg = sb("agg", [P, NT, D + 1])
        conv = sb("conv", [P, NT, HID])
        z_sb = sb("z_sb", [P, NT, HID])
        dinv = sb("dinv", [P, NT])
        edges = sb("edges", [P, 2, TILES, D])
        gathered = sb("gathered", [P, 2, TILES, D])
        ident = sb("ident", [P, P])
        iota_i = sb("iota_i", [P, P], I32)
        iota = sb("iota", [P, P])
        base_i = sb("base_i", [P, NT], I32)
        node_base = sb("node_base", [P, NT])
        ones = sb("ones", [P, 1])
        zero = sb("zero", [P, 1])
        zeros = sb("zeros", [P, 1, D + 1])
        eps = sb("eps", [P, 1])
        wm_top, wm_bot = sb("wm_top", [P, D]), sb("wm_bot", [P, D])
        wu_top, wu_bot = sb("wu_top", [P, D]), sb("wu_bot", [P, D])
        w1_sb, w2_sb = sb("w1_sb", [P, HID]), sb("w2_sb", [HID, D])
        bm_sb, bu_sb, gm_sb, be_sb, b2_sb = (sb(n, [P, D]) for n in ("bm_sb", "bu_sb", "gm_sb", "be_sb", "b2_sb"))
        b1_sb = sb("b1_sb", [P, HID])
        starts_f = sb("starts_f", [1, NT])
        starts = sb("starts", [1, NT], I32)
        miss_f = sb("miss_f", [1, 1])
        miss = sb("miss", [1, 1], I32)
        cnt_col = sb("cnt_col", [P, 1])
        rows = sb("rows", [P, 2, 2, TILES], I32)
        src_idx = [sb(f"src_idx{q}", [P, TILES], I32) for q in range(2)]
        dst_loc = sb("dst_loc", [P, 2, TILES])
        edges_T = sb("edges_T", [P, 2, 512])
        pre = sb("pre", [P, 2, 512])
        msgs = sb("msgs", [P, 2, GT, D + 1])
        hot = sb("hot", [P, 2, GT, P])
        stat = sb("stat", [P, 4, BT])
        bt0, bt1, bt2, bt3 = (sb(f"bt{i}", [P, BT, D]) for i in range(4))

        bank = [ctx.enter_context(nc.psum_tensor(f"bank{i}", [P, 512], F32)) for i in range(8)]

        def wide(ap, n=D):
            return ap.unsqueeze(2).to_broadcast([ap.shape[0], ap.shape[1], n])

        def over(ap, k):
            return ap.unsqueeze(1).to_broadcast([ap.shape[0], k, ap.shape[1]])

        def halves(a, b, n, w=D):
            per = 512 // D
            return [(bank[(a, b)[t // per]][:, (t % per) * w:(t % per) * w + w]) for t in range(n)]

        def block_of(a, k, w=D):
            return bank[a][:, 0:k * w].rearrange("p (t f) -> p t f", f=w)

        s_x, s_w, s_dst, s_pad, s_any = (phase_sem(n) for n in ("x_loaded", "weights_loaded", "dst_loaded", "pad_set",
                                                               "dst_any_written"))
        s_pc, s_vc, s_col, s_st = (phase_sem(n) for n in ("pool_consts", "vector_steps", "counts_summed", "starts_set"))
        dst_i = edges[0:SP_, 0, :, :].rearrange("p t f -> p (t f)").bitcast(I32)[:, 0:PER]
        below = gathered[0:SP_, :, :, :].rearrange("p q t f -> p (q t f)")[:, 0:NT * (PER // STRIDE)]\
            .rearrange("p (n k) -> p n k", n=NT)
        n_below = agg[0:SP_, 0, 0:NT]
        pad = base_i[0:1, :]
        PAD = CHUNKS * CHUNK - E
        HEAD = (CHUNKS - 1) * CHUNK

        with nc.Block() as block:
            @block.sync
            def _(sp):
                sp.dma_start(dst_i, dst.rearrange("(p k) -> p k", p=SP_)).then_inc(s_dst, 16)
                for k in range(NB):
                    hi = min((k + 1) * BT, FULL)
                    sp.dma_start(x_sb[:, k * BT:hi, :],
                                 x[k * BT * P:hi * P, :].rearrange("(t p) f -> p t f", p=P)).then_inc(s_x, 16)
                sp.wait_ge(s_vc, 1)
                sp.dma_start(x_sb[0:TAIL, FULL, :], x[FULL * P:N, :]).then_inc(s_x, 16)
                sp.dma_start(dst_any[0:HEAD].rearrange("(a b) -> a b", a=CHUNKS - 1),
                             dst[0:HEAD].rearrange("(a b) -> a b", a=CHUNKS - 1)).then_inc(s_any, 16)
                sp.dma_start(dst_any[HEAD + PAD:], dst[HEAD:]).then_inc(s_any, 16)
                sp.wait_ge(s_pad, 1)
                at = HEAD
                while at < HEAD + PAD:
                    n = min(NT, HEAD + PAD - at)
                    sp.dma_start(dst_any[at:at + n].unsqueeze(0), pad[:, 0:n]).then_inc(s_any, 16)
                    at += n
                sp.wait_ge(s_any, 16 * (2 + -(-PAD // NT)))
                sp.wait_ge(s_x, 16 * (NB + 1))
                sp.wait_ge(s_dst, 16)

            @block.scalar
            def _(act):
                for n, (to, of) in enumerate([
                        (wm_top, W_msg[0:D, :]), (wm_bot, W_msg[D:, :]), (wu_top, W_upd[0:D, :]),
                        (wu_bot, W_upd[D:, :]), (w1_sb, W1), (w2_sb, W2)]):
                    act.dma_start(to[:, :], of).then_inc(s_w, 16)
                for to, of in ((bm_sb, b_msg), (bu_sb, b_upd), (gm_sb, gamma), (be_sb, beta), (b2_sb, b2), (b1_sb, b1)):
                    act.dma_start(to[:, :], of.partition_broadcast(P)).then_inc(s_w, 16)
                act.wait_ge(s_w, 16 * 12)

            @block.gpsimd
            def _(pool):
                pool.memset(ident[:, :], 0.0).then_inc(s_pc, 1)
                pool.wait_ge(s_pc, 1)
                pool.affine_select(out=ident[:, :], in_=ident[:, :], compare_op=ALU.not_equal, fill=1.0, base=0,
                                   pattern=[[-1, P]], channel_multiplier=1).then_inc(s_pc, 1)
                pool.iota(iota_i[:, :], pattern=[[1, P]], base=0, channel_multiplier=0).then_inc(s_pc, 1)
                pool.iota(base_i[:, :], pattern=[[P, NT]], base=0, channel_multiplier=0).then_inc(s_pc, 1)
                pool.wait_ge(s_vc, 3)
                pool.memset(pad, -1).then_inc(s_pad, 1)

            @block.vector
            def _(dve):
                dve.memset(x_sb[:, FULL, :], 0.0).then_inc(s_vc, 1)
                dve.memset(ones[:, :], 1.0).then_inc(s_vc, 1)
                dve.memset(zero[:, :], 0.0)
                dve.memset(eps[:, :], EPS)
                dve.memset(zeros[:, :, :], 0.0)
                dve.memset(msgs[:, :, :, D:D + 1], 1.0)
                dve.wait_ge(s_pc, 4)
                dve.tensor_copy(iota[:, :], iota_i[:, :])
                dve.tensor_copy(node_base[:, :], base_i[:, :]).then_inc(s_vc, 1)
                dve.wait_ge(s_vc, 3)
                dve.wait_ge(s_dst, 16)
                k = PER // STRIDE
                every = dst_i.rearrange("p (k s) -> p k s", s=STRIDE)[:, :, 0]
                dve.tensor_tensor(below, every.unsqueeze(1).to_broadcast([SP_, NT, k]),
                                  node_base[0:SP_, :].unsqueeze(2).to_broadcast([SP_, NT, k]), ALU.is_lt)\
                   .then_inc(s_vc, 1)
                dve.wait_ge(s_vc, 4)
                dve.tensor_reduce(n_below, below, AX.X, ALU.add).then_inc(s_vc, 1)
                dve.wait_ge(s_col, 1)
                dve.tensor_scalar(starts_f[:, :], bank[0][0:1, 0:NT], float(STRIDE), float(-STRIDE), ALU.mult, ALU.add)\
                   .then_inc(s_vc, 1)
                dve.wait_ge(s_vc, 6)
                dve.tensor_scalar(starts[:, :], starts_f[:, :], 0.0, float(LAST_START), ALU.max, ALU.min)\
                   .then_inc(s_st, 1)

            @block.tensor
            def _(pe):
                pe.wait_ge(s_vc, 5)
                pe.matmul(bank[0][0:1, 0:NT], ones[0:SP_, :], n_below, start=True, stop=True).then_inc(s_col, 1)
        clear(used)
        used.clear()

        s_v = sem("vector_steps_b")
        s_var = sem("variance_ready")
        s_std = sem("deviation_ready")
        s_tr = sem("transposes_done")
        s_ev = sem("transposes_copied")
        s_mm = sem("products_done")
        s_res = sem("result_ready")
        s_st = sem("result_stored")
        dense_sems = [s_v, s_var, s_std, s_tr, s_ev, s_mm, s_res, s_st]

        class Chain:
            def __init__(self, eng, s):
                self.eng, self.s, self.n = eng, s, 0

            def __call__(self, ins):
                self.n += 1
                ins.then_inc(self.s, 1)
                self.eng.wait_ge(self.s, self.n)

        def normalize(dve, step, of, to, scratch, nth):
            step(dve.tensor_reduce(stat[:, 0, :], of, AX.X, ALU.add))
            step(dve.tensor_scalar(stat[:, 1, :], stat[:, 0, :], -1.0 / D, None, ALU.mult))
            step(dve.tensor_tensor(to, of, wide(stat[:, 1, :]), ALU.add))
            step(dve.tensor_tensor(scratch, to, to, ALU.mult))
            step(dve.tensor_reduce(stat[:, 0, :], scratch, AX.X, ALU.add))
            dve.tensor_scalar(stat[:, 2, :], stat[:, 0, :], 1.0 / D, None, ALU.mult).then_inc(s_var, 1)
            dve.wait_ge(s_std, nth)
            step(dve.reciprocal(stat[:, 1, :], stat[:, 3, :]))
            step(dve.tensor_tensor(to, to, wide(stat[:, 1, :]), ALU.mult))

        def deviation(act, nth):
            act.wait_ge(s_var, nth)
            act.activation(stat[:, 3, :], stat[:, 2, :], ACT.Sqrt, bias=eps[:, 0:1]).then_inc(s_std, 1)

        def transpose_batch(pe, of, a, b):
            for t, place in enumerate(halves(a, b, BT)):
                last = pe.transpose(place, of[:, t, :], ident[:, :])
            return last

        def copy_batch(act, to, a, b):
            act.copy(to[:, 0:GT, :], block_of(a, GT))
            return act.copy(to[:, GT:BT, :], block_of(b, BT - GT))

        def add_banks(dve, step, to, a, b, row):
            dve.tensor_tensor(to[:, 0:GT, :], block_of(a, GT), over(row[:, :], GT), ALU.add)
            step(dve.tensor_tensor(to[:, GT:BT, :], block_of(b, BT - GT), over(row[:, :], BT - GT), ALU.add))

        with nc.Fori(0, NB) as i:
            tiles = bass.ds(i * BT, BT)
            with nc.Block() as block:
                @block.vector
                def _(dve):
                    step = Chain(dve, s_v)
                    normalize(dve, step, x_sb[:, tiles, :], bt0[:, :, :], bt1[:, :, :], 1)
                    step(dve.tensor_scalar(h_sb[:, tiles, :], bt0[:, :, :], 0.0, None, ALU.max))
                    dve.tensor_copy(bt0[:, :, :], h_sb[:, tiles, :]).then_inc(s_res, 1)
                    dve.wait_ge(s_mm, 1)
                    add_banks(dve, step, bt2, 2, 3, bm_sb)
                    dve.wait_ge(s_v, step.n)
                    dve.memset(stat[:, 0, 0:1], 0.0).then_inc(s_res, 1)

                @block.scalar
                def _(act):
                    deviation(act, 1)
                    act.wait_ge(s_tr, 1)
                    copy_batch(act, bt1, 0, 1).then_inc(s_ev, 1)

                @block.tensor
                def _(pe):
                    pe.wait_ge(s_res, 1)
                    transpose_batch(pe, bt0, 0, 1).then_inc(s_tr, 1)
                    pe.wait_ge(s_ev, 1)
                    for t, place in enumerate(halves(2, 3, BT)):
                        last = pe.matmul(place, bt1[:, t, :], wm_top[:, :], start=True, stop=True)
                    last.then_inc(s_mm, 1)

                @block.sync
                def _(sp):
                    sp.wait_ge(s_res, 2)
                    sp.dma_start(y_table[bass.ds(i * BT * P, BT * P), :].rearrange("(t p) f -> p t f", p=P),
                                 bt2[:, :, :]).then_inc(s_st, 16)
                    sp.wait_ge(s_st, 16)
            clear(dense_sems)

        g_names = ("rows_loaded", "edges_loaded", "src_ready", "rows_gathered",
                   "hot_ready", "edges_transposed", "edges_copied", "products", "messages", "scattered", "chunk_steps",
                   "summed")
        g = {n: sem("g_" + n) for n in g_names}

        def chunk_block(kind, table, start, dst_rows, node):
            width = D if kind == "message" else HID
            to = gathered[:, 0, :, 0:width] if kind == "message" else \
                gathered[:, 0, :, :].rearrange("p t f -> p (t f)")[:, 0:TILES * HID].rearrange("p (t f) -> p t f", f=HID)
            with nc.Block() as block:
                @block.sync
                def _(sp):
                    s = start(sp)
                    sp.dma_start(rows[:, 0, 0, :], src[bass.ds(s, CHUNK)].rearrange("(p j) -> p j", p=P))\
                      .then_inc(g["rows_loaded"], 16)
                    sp.dma_start(rows[:, 0, 1, :], dst_rows(s)).then_inc(g["rows_loaded"], 16)
                    if kind == "message":
                        sp.dma_start(edges[:, 0, :, :].rearrange("p j f -> p (j f)"),
                                     edge_attr[bass.ds(s, CHUNK), :].rearrange("(p j) f -> p (j f)", p=P))\
                          .then_inc(g["edges_loaded"], 16)

                @block.gpsimd
                def _(pool):
                    pool.wait_ge(g["src_ready"], 1)
                    for j in range(TILES):
                        pool.indirect_dma_start(to[:, j, :], None, table[:, :],
                                                bass.IndirectOffsetOnAxis(ap=src_idx[0][:, j:j + 1], axis=0))\
                            .then_inc(g["rows_gathered"], 16)
                    pool.wait_ge(g["rows_gathered"], 16 * TILES)

                @block.vector
                def _(dve):
                    step = Chain(dve, g["chunk_steps"])
                    dve.wait_ge(g["rows_loaded"], 32)
                    dve.tensor_copy(src_idx[0][:, :], rows[:, 0, 0, :]).then_inc(g["src_ready"], 1)
                    step(dve.tensor_tensor(dst_loc[:, 0, :], rows[:, 0, 1, :],
                                           node_base[:, bass.ds(node, 1)].to_broadcast([P, TILES]), ALU.subtract))
                    for n, (j, k) in enumerate(GROUPS):
                        if n:
                            dve.wait_ge(g["scattered"], n)
                        dve.tensor_tensor(hot[:, 0, 0:k, :], over(iota[:, :], k), wide(dst_loc[:, 0, j:j + k], P),
                                          ALU.is_equal).then_inc(g["hot_ready"], 1)
                        if n == 0:
                            dve.wait_ge(g["rows_gathered"], 16 * TILES)
                        if kind == "message":
                            dve.wait_ge(g["products"], n + 1)
                            pr = pre[:, 0, 0:k * D].rearrange("p (t f) -> p t f", f=D)
                            step(dve.tensor_tensor(pr, block_of(1, k), to[:, j:j + k, :], ALU.add))
                            dve.tensor_scalar(msgs[:, 0, 0:k, 0:D], pr, 0.0, None, ALU.max).then_inc(g["messages"], 1)
                    dve.wait_ge(g["scattered"], NG)
                    sums = agg if kind == "message" else conv
                    n = sums.shape[2]
                    dve.tensor_tensor(sums[:, bass.ds(node, 1), :].rearrange("p a f -> p (a f)"),
                                      sums[:, bass.ds(node, 1), :].rearrange("p a f -> p (a f)"),
                                      bank[4][:, 0:n], ALU.add).then_inc(g["summed"], 1)

                @block.scalar
                def _(act):
                    if kind == "message":
                        for n, (j, k) in enumerate(GROUPS):
                            act.wait_ge(g["edges_transposed"], n + 1)
                            act.copy(edges_T[:, 0, 0:k * P], bank[0][:, 0:k * P]).then_inc(g["edges_copied"], 1)

                @block.tensor
                def _(pe):
                    if kind == "message":
                        pe.wait_ge(g["edges_loaded"], 16)
                    else:
                        pe.wait_ge(g["rows_gathered"], 16 * TILES)
                    for n, (j, k) in enumerate(GROUPS):
                        if kind == "message":
                            for t in range(k):
                                last = pe.transpose(bank[0][:, t * P:t * P + P], edges[:, 0, j + t, :], ident[:, :])
                            last.then_inc(g["edges_transposed"], 1)
                            pe.wait_ge(g["edges_copied"], n + 1)
                            for t in range(k):
                                last = pe.matmul(bank[1][:, t * D:t * D + D], edges_T[:, 0, t * P:t * P + P],
                                                 wm_bot[:, :], start=True, stop=True)
                            last.then_inc(g["products"], 1)
                            pe.wait_ge(g["messages"], n + 1)
                        pe.wait_ge(g["hot_ready"], n + 1)
                        for t in range(k):
                            rhs = msgs[:, 0, t, :] if kind == "message" else to[:, j + t, :]
                            last = pe.matmul(bank[4][:, 0:rhs.shape[1]], hot[:, 0, t, :], rhs,
                                             start=j + t == 0, stop=j + t == TILES - 1)
                        last.then_inc(g["scattered"], 1)
            nc.gpsimd.dma_reset(range(g["rows_gathered"].num, g["rows_gathered"].num + 1))
            clear(list(g.values()))

        def set_zero(sums):
            with nc.Block() as block:
                @block.vector
                def _(dve):
                    dve.memset(sums[:, :, :], 0.0)

        def pass_by_tile(kind, table):
            set_zero(agg if kind == "message" else conv)
            with nc.Fori(0, NT) as i:
                chunk_block(kind, table,
                            lambda sp: sp.value_load(starts[0:1, bass.ds(i, 1)], min_val=0, max_val=LAST_START),
                            lambda s: dst[bass.ds(s, CHUNK)].rearrange("(p j) -> p j", p=P), i)

        def pass_over_all(kind, table):
            with nc.Fori(0, NT) as i:
                with nc.Block() as block:
                    @block.vector
                    def _(dve):
                        sums = (agg if kind == "message" else conv)[:, bass.ds(i, 1), :]
                        dve.tensor_copy(sums, zeros[:, :, 0:sums.shape[2]])
                with nc.Fori(0, CHUNKS - 1) as c:
                    chunk_block(kind, table, lambda sp: c * CHUNK,
                                lambda s: dst_any[bass.ds(s, CHUNK)].rearrange("(p j) -> p j", p=P), i)
                chunk_block(kind, table, lambda sp: LAST_START,
                            lambda s: dst_any[HEAD:HEAD + CHUNK].rearrange("(p j) -> p j", p=P), i)

        pass_by_tile("message", y_table)

        s_c, s_m = sem("counts_column"), sem("miss_summed")
        s_ms = sem("miss_set")
        with nc.Block() as block:
            @block.vector
            def _(dve):
                dve.tensor_reduce(cnt_col[:, :], agg[:, :, D:D + 1].rearrange("p n a -> p (n a)"), AX.X, ALU.add)\
                   .then_inc(s_c, 1)
                dve.wait_ge(s_m, 1)
                dve.tensor_scalar(miss[:, :], bank[0][0:1, 0:1], -1.0, float(E), ALU.mult, ALU.add).then_inc(s_ms, 1)
                dve.wait_ge(s_ms, 1)

            @block.tensor
            def _(pe):
                pe.wait_ge(s_c, 1)
                pe.matmul(bank[0][0:1, 0:1], ones[:, :], cnt_col[:, :], start=True, stop=True).then_inc(s_m, 1)
        missed = nc.values_load(miss[0:1, 0:1], min_val=0, max_val=E)
        with nc.If(missed != 0):
            pass_over_all("message", y_table)

        with nc.Fori(0, NB) as i:
            tiles = bass.ds(i * BT, BT)
            counts = agg[:, tiles, D:D + 1].rearrange("p n a -> p (n a)")
            with nc.Block() as block:
                @block.vector
                def _(dve):
                    step = Chain(dve, s_v)
                    step(dve.tensor_scalar(stat[:, 0, :], counts, 1.0, None, ALU.max))
                    step(dve.reciprocal(stat[:, 1, :], stat[:, 0, :]))
                    step(dve.tensor_tensor(bt0[:, :, :], agg[:, tiles, 0:D], wide(stat[:, 1, :]), ALU.mult))
                    dve.tensor_copy(bt1[:, :, :], h_sb[:, tiles, :]).then_inc(s_res, 1)
                    dve.wait_ge(s_mm, 1)
                    add_banks(dve, step, bt0, 4, 5, bu_sb)
                    normalize(dve, step, bt0[:, :, :], bt1[:, :, :], bt2[:, :, :], 1)
                    step(dve.tensor_tensor(bt1[:, :, :], bt1[:, :, :], over(gm_sb[:, :], BT), ALU.mult))
                    step(dve.tensor_tensor(bt1[:, :, :], bt1[:, :, :], over(be_sb[:, :], BT), ALU.add))
                    step(dve.tensor_tensor(bt1[:, :, :], bt1[:, :, :], h_sb[:, tiles, :], ALU.add))
                    step(dve.tensor_scalar(bt1[:, :, :], bt1[:, :, :], 0.0, None, ALU.max))
                    step(dve.tensor_tensor(x_sb[:, tiles, :], x_sb[:, tiles, :], bt1[:, :, :], ALU.add))
                    normalize(dve, step, x_sb[:, tiles, :], bt0[:, :, :], bt2[:, :, :], 2)
                    step(dve.tensor_scalar(stat[:, 2, :], counts, 1.0, None, ALU.add))
                    dve.tensor_scalar(bt0[:, :, :], bt0[:, :, :], 0.0, None, ALU.max).then_inc(s_res, 1)
                    dve.wait_ge(s_std, 3)
                    step(dve.reciprocal(dinv[:, tiles], stat[:, 3, :]))
                    dve.wait_ge(s_mm, 2)
                    step(dve.tensor_tensor(z_sb[:, tiles, :], block_of(6, BT, HID), wide(dinv[:, tiles], HID), ALU.mult))

                @block.scalar
                def _(act):
                    act.wait_ge(s_tr, 1)
                    copy_batch(act, bt2, 0, 1)
                    copy_batch(act, bt3, 2, 3).then_inc(s_ev, 1)
                    deviation(act, 1)
                    deviation(act, 2)
                    act.wait_ge(s_res, 2)
                    act.activation(stat[:, 3, :], stat[:, 2, :], ACT.Sqrt, bias=zero[:, 0:1]).then_inc(s_std, 1)
                    act.wait_ge(s_tr, 2)
                    copy_batch(act, bt1, 0, 1).then_inc(s_ev, 1)

                @block.tensor
                def _(pe):
                    pe.wait_ge(s_res, 1)
                    transpose_batch(pe, bt0, 0, 1)
                    transpose_batch(pe, bt1, 2, 3).then_inc(s_tr, 1)
                    pe.wait_ge(s_ev, 1)
                    for t, place in enumerate(halves(4, 5, BT)):
                        pe.matmul(place, bt3[:, t, :], wu_top[:, :], start=True, stop=False)
                        last = pe.matmul(place, bt2[:, t, :], wu_bot[:, :], start=False, stop=True)
                    last.then_inc(s_mm, 1)
                    pe.wait_ge(s_res, 2)
                    transpose_batch(pe, bt0, 0, 1).then_inc(s_tr, 1)
                    pe.wait_ge(s_ev, 2)
                    for t in range(BT):
                        last = pe.matmul(bank[6][:, t * HID:(t + 1) * HID], bt1[:, t, :], w1_sb[:, :],
                                         start=True, stop=True)
                    last.then_inc(s_mm, 1)
            clear(dense_sems)

        def table_rows(table):
            return table[:, :].rearrange("(t p) f -> p t f", p=P)

        def store_z(table):
            with nc.Block() as block:
                @block.sync
                def _(sp):
                    sp.dma_start(table_rows(table), z_sb[:, :, :]).then_inc(s_st, 16)
                    sp.wait_ge(s_st, 16)
            clear([s_st])

        def convolve(table):
            pass_by_tile("row", table)
            with nc.If(missed != 0):
                pass_over_all("row", table)

        store_z(z1_table)
        convolve(z1_table)
        with nc.Block() as block:
            @block.vector
            def _(dve):
                step = Chain(dve, s_v)
                step(dve.tensor_tensor(conv[:, :, :], conv[:, :, :], z_sb[:, :, :], ALU.add))
                step(dve.tensor_tensor(conv[:, :, :], conv[:, :, :], wide(dinv[:, :], HID), ALU.mult))
                step(dve.tensor_tensor(conv[:, :, :], conv[:, :, :], over(b1_sb[:, :], NT), ALU.add))
                step(dve.tensor_scalar(conv[:, :, :], conv[:, :, :], 0.0, None, ALU.max))
                step(dve.tensor_tensor(z_sb[:, :, :], conv[:, :, :], wide(dinv[:, :], HID), ALU.mult))
        clear(dense_sems)

        store_z(z2_table)
        convolve(z2_table)
        with nc.Block() as block:
            @block.vector
            def _(dve):
                step = Chain(dve, s_v)
                step(dve.tensor_tensor(conv[:, :, :], conv[:, :, :], z_sb[:, :, :], ALU.add))
                step(dve.tensor_tensor(conv[:, :, :], conv[:, :, :], wide(dinv[:, :], HID), ALU.mult))
        clear(dense_sems)
        with nc.Fori(0, NB) as i:
            tiles = bass.ds(i * BT, BT)
            with nc.Block() as block:
                @block.vector
                def _(dve):
                    dve.tensor_copy(bt0[:, :, 0:HID], conv[:, tiles, :]).then_inc(s_res, 1)
                    dve.wait_ge(s_mm, 1)
                    step = Chain(dve, s_v)
                    add_banks(dve, step, bt2, 2, 3, b2_sb)
                    step(dve.tensor_tensor(x_sb[:, tiles, :], x_sb[:, tiles, :], bt2[:, :, :], ALU.add))

                @block.tensor
                def _(pe):
                    pe.wait_ge(s_res, 1)
                    for t, place in enumerate(halves(0, 1, BT)):
                        last = pe.transpose(place[0:HID, :], bt0[:, t, 0:HID], ident[:, :])
                    last.then_inc(s_tr, 1)
                    pe.wait_ge(s_ev, 1)
                    for t, place in enumerate(halves(2, 3, BT)):
                        last = pe.matmul(place, bt1[0:HID, t, :], w2_sb[:, :], start=True, stop=True)
                    last.then_inc(s_mm, 1)

                @block.scalar
                def _(act):
                    act.wait_ge(s_tr, 1)
                    act.copy(bt1[0:HID, 0:GT, :], block_of(0, GT)[0:HID])
                    act.copy(bt1[0:HID, GT:BT, :], block_of(1, BT - GT)[0:HID]).then_inc(s_ev, 1)
            clear(dense_sems)
        with nc.Block() as block:
            @block.sync
            def _(sp):
                sp.dma_start(out[0:FULL * P, :].rearrange("(t p) f -> p t f", p=P), x_sb[:, 0:FULL, :])\
                  .then_inc(s_st, 16)
                sp.dma_start(out[FULL * P:N, :], x_sb[0:TAIL, FULL, :]).then_inc(s_st, 16)
                sp.wait_ge(s_st, 32)


_INS = ["x", "src", "dst", "edge_attr_128", "L0_gnn_W_msg", "L0_gnn_b_msg", "L0_gnn_W_upd", "L0_gnn_b_upd",
        "L0_gnn_gamma", "L0_gnn_beta", "L1_gnn_W1", "L1_gnn_b1", "L1_gnn_W2", "L1_gnn_b2"]


def kernel(**inputs):
    import numpy as _np
    import concourse.bacc as _bacc
    from concourse import mybir as _mybir
    from concourse.bass_utils import run_bass_kernel_spmd as _run

    nc = _bacc.Bacc("TRN2", target_bir_lowering=False, num_devices=1)
    arrays, args = {}, []
    for name in _INS:
        a = _np.ascontiguousarray(inputs[name])
        arrays[f"in_{name}"] = a
        args.append(nc.dram_tensor(f"in_{name}", a.shape, _mybir.dt.from_np(a.dtype), kind="ExternalInput").ap())
    args.append(nc.dram_tensor("out_nodes", arrays["in_x"].shape, _mybir.dt.float32, kind="ExternalOutput").ap())
    gnn_kernel(nc, *args)
    r = _run(nc, [arrays], core_ids=[0])
    return r.results[0]["out_nodes"]
```

```python
import concourse.bass as bass
from concourse import mybir
from contextlib import ExitStack

F32 = mybir.dt.float32
I32 = mybir.dt.int32
F16 = mybir.dt.float16
BF16 = mybir.dt.bfloat16
FP8 = mybir.dt.float8e4
U8 = mybir.dt.uint8
ALU = mybir.AluOpType
ACT = mybir.ActivationFunctionType
AX = mybir.AxisListType
P = 128
EPS = 1e-5


def gnn_kernel(nc, x, src, dst, edge_attr, W_msg, b_msg, W_upd, b_upd, gamma, beta, W1, b1, W2, b2, out):
    N, D = x.shape
    E = src.shape[0]
    HID = W1.shape[1]
    NT = -(-N // P)
    FULL = N // P
    TAIL = N - FULL * P
    TILES = -(-E // N) + 2
    CHUNK = TILES * P
    GT = 512 // D
    GROUPS = [(g, min(GT, TILES - g)) for g in range(0, TILES, GT)]
    NG = len(GROUPS)
    LAST_START = E - CHUNK
    CHUNKS = -(-E // CHUNK)
    BT = 7 if NT % 7 == 0 else 5
    NB = NT // BT
    assert NT % BT == 0 and NT % 2 == 1
    SUB = 16
    WINDOWS = P // SUB
    WK = -(-(SUB * E // N) // P) + 1
    WEDGES = WK * P
    CELLS = NT * SUB
    HALVES = [(0, (NT + 1) // 2 * SUB), ((NT + 1) // 2 * SUB, CELLS)]
    EXACT = 16.0
    PARTS = 3
    FIELDS = 3
    QT = 4
    QUADS = NT // QT
    SP_ = 125
    STRIDE = 16
    PER = E // SP_
    assert PER % STRIDE == 0 and D == P

    ctx = ExitStack()
    with ctx:
        def sb(name, shape, dt=F32):
            return ctx.enter_context(nc.sbuf_tensor(name, shape, dt))

        def sem(name):
            return ctx.enter_context(nc.semaphore(name))

        used = []

        def phase_sem(name):
            s = sem(name)
            used.append(s)
            return s

        def clear(sems):
            for s in sems:
                nc.sync.sem_clear(s)
            nc.all_engine_barrier()

        y_table = nc.dram_tensor("y_table", [NT * P, D], F32)
        z1_table = nc.dram_tensor("z1_table", [NT * P, HID], F32)
        z2_table = nc.dram_tensor("z2_table", [NT * P, HID], F32)
        adjacency = nc.dram_tensor("adjacency", [NT, P, WINDOWS * CELLS], U8)
        fields = nc.dram_tensor("fields", [E, FIELDS], F32)
        dst_any = nc.dram_tensor("dst_any", [CHUNKS * CHUNK], I32)

        x_sb = sb("x_sb", [P, NT, D])
        h_sb = sb("h_sb", [P, NT, D])
        agg = sb("agg", [P, NT, D + 1])
        conv = sb("conv", [P, NT, HID])
        z_sb = sb("z_sb", [P, NT, HID])
        dinv = sb("dinv", [P, NT])
        work = sb("work", [P, 4, TILES * D])
        edges = work[:, 0:2, :].rearrange("p q (t f) -> p q t f", f=D)
        gathered = work[:, 2:4, :].rearrange("p q (t f) -> p q t f", f=D)
        ident = sb("ident", [P, P])
        iota_i = z_sb[:, :, :].rearrange("p n f -> p (n f)").bitcast(I32)[:, 0:P]
        iota = sb("iota", [P, P])
        base_i = sb("base_i", [P, NT], I32)
        node_base = sb("node_base", [P, NT])
        ones = sb("ones", [P, 1])
        zero = sb("zero", [P, 1])
        zeros = sb("zeros", [P, 1, D + 1])
        eps = sb("eps", [P, 1])
        wm_top, wm_bot = sb("wm_top", [P, D]), sb("wm_bot", [P, D])
        wu_top, wu_bot = sb("wu_top", [P, D]), sb("wu_bot", [P, D])
        w1_sb, w2_sb = sb("w1_sb", [P, HID]), sb("w2_sb", [HID, D])
        bm_sb, bu_sb, gm_sb, be_sb, b2_sb = (sb(n, [P, D]) for n in ("bm_sb", "bu_sb", "gm_sb", "be_sb", "b2_sb"))
        b1_sb = sb("b1_sb", [P, HID])
        starts_f = sb("starts_f", [1, NT * WINDOWS])
        window_starts = sb("window_starts", [1, NT * WINDOWS], I32)
        starts = sb("starts", [1, NT], I32)
        miss = sb("miss", [1, 2], I32)
        miss_col = sb("miss_col", [P, 3])
        rows = sb("rows", [P, 2, 2, TILES], I32)
        keys = sb("keys", [P, 2, WINDOWS, WK, FIELDS])
        window_base = sb("window_base", [P, WINDOWS, WK])
        window_i = sb("window_i", [P, WINDOWS, WK], I32)
        cell_i = conv[:, :, :].rearrange("p n f -> p (n f)").bitcast(I32)[:, 0:CELLS]
        cell_key = sb("cell_key", [P, CELLS], F16)
        iota_b = sb("iota_b", [P, P], BF16)
        key_tmp = sb("key_tmp", [P, 2, WINDOWS, WK])
        cell_of = sb("cell_of", [P, 2, WINDOWS, WK])
        src_low = sb("src_low", [P, 2, WINDOWS, WK], BF16)
        cell_hot = sb("cell_hot", [P, 2, WK, CELLS], BF16)
        low_hot = sb("low_hot", [P, 2, WK, P], BF16)
        cells = sb("cells", [P, WINDOWS * CELLS], FP8)
        over_junk = sb("over_junk", [P, 2, HALVES[0][1]], BF16)
        assert HID >= SUB
        tally = sb("tally", [P, 2, 2, 2 * WINDOWS])
        tallies = sb("tallies", [P, 2, NT, 2 * WINDOWS])
        neg_exact = sb("neg_exact", [P, 1])
        fold = sb("fold", [PARTS * HID, HID])
        parts = h_sb[:, :, :].rearrange("p n f -> p (n f)").bitcast(BF16)[:, 0:NT * PARTS * HID]\
            .rearrange("p (n c f) -> p n c f", c=PARTS, f=HID)
        dst_loc = sb("dst_loc", [P, 2, TILES])
        edges_T = sb("edges_T", [P, 2, 512])
        part_sums = edges_T[0:PARTS * HID, :, 0:QT * P]
        msgs = sb("msgs", [P, 2, GT, D + 1])
        hot = sb("hot", [P, 2, GT, P])
        stat = sb("stat", [P, 4, BT])
        bt0, bt1, bt2, bt3 = (work[:, 1, i * BT * D:(i + 1) * BT * D].rearrange("p (t f) -> p t f", f=D)
                              for i in range(4))

        bank = [ctx.enter_context(nc.psum_tensor(f"bank{i}", [P, 512], F32)) for i in range(8)]

        def wide(ap, n=D):
            return ap.unsqueeze(2).to_broadcast([ap.shape[0], ap.shape[1], n])

        def over(ap, k):
            return ap.unsqueeze(1).to_broadcast([ap.shape[0], k, ap.shape[1]])

        def halves(a, b, n, w=D):
            per = 512 // D
            return [(bank[(a, b)[t // per]][:, (t % per) * w:(t % per) * w + w]) for t in range(n)]

        def block_of(a, k, w=D):
            return bank[a][:, 0:k * w].rearrange("p (t f) -> p t f", f=w)

        s_x, s_w, s_dst, s_pad, s_any = (phase_sem(n) for n in ("x_loaded", "weights_loaded", "dst_loaded", "pad_set",
                                                               "dst_any_written"))
        s_pc, s_vc, s_col, s_st = (phase_sem(n) for n in ("pool_consts", "vector_steps", "counts_summed", "starts_set"))
        room = work[0:SP_, :, :].rearrange("p q n -> p (q n)")
        src_i = room[:, 0:PER].bitcast(I32)
        dst_i = room[:, PER:2 * PER].bitcast(I32)
        field_f = room[:, 2 * PER:(2 + FIELDS) * PER].rearrange("p (k c) -> p k c", c=FIELDS)
        high_i = room[:, (2 + FIELDS) * PER:(3 + FIELDS) * PER].bitcast(I32)
        assert (3 + FIELDS) * PER <= 4 * TILES * D
        SAMPLES = PER // STRIDE
        sample_i = agg[0:SP_, 0, 0:SAMPLES].bitcast(I32)
        sample_f = agg[0:SP_, 1, 0:SAMPLES]
        NW = NT * WINDOWS
        SB = 5
        less = cell_hot[0:SP_, :, :, :].rearrange("p q k c -> p (q k c)")[:, 0:2 * SB * NW]\
            .rearrange("p (q s n) -> p q s n", q=2, s=SB)
        ones_b = low_hot[0:SP_, 0, 0, 0:1]
        window_no = low_hot.bitcast(F16)[0:SP_, 1, :, :].rearrange("p k n -> p (k n)")[:, 0:NW]
        assert SAMPLES % SB == 0 and NW <= WK * P and 2 * SB * NW <= 2 * WK * CELLS and SAMPLES <= D + 1
        pad = base_i[0:1, :]
        PAD = CHUNKS * CHUNK - E
        HEAD = (CHUNKS - 1) * CHUNK
        s_src, s_f, s_fs, s_less, s_sum = (phase_sem(n) for n in ("src_loaded", "fields_ready", "fields_stored",
                                                                  "less_ready", "samples_summed"))

        with nc.Block() as block:
            @block.sync
            def _(sp):
                sp.dma_start(dst_i, dst.rearrange("(p k) -> p k", p=SP_)).then_inc(s_dst, 16)
                sp.dma_start(src_i, src.rearrange("(p k) -> p k", p=SP_)).then_inc(s_src, 16)
                for k in range(NB):
                    hi = min((k + 1) * BT, FULL)
                    sp.dma_start(x_sb[:, k * BT:hi, :],
                                 x[k * BT * P:hi * P, :].rearrange("(t p) f -> p t f", p=P)).then_inc(s_x, 16)
                sp.wait_ge(s_vc, 1)
                sp.dma_start(x_sb[0:TAIL, FULL, :], x[FULL * P:N, :]).then_inc(s_x, 16)
                sp.dma_start(dst_any[0:HEAD].rearrange("(a b) -> a b", a=CHUNKS - 1),
                             dst[0:HEAD].rearrange("(a b) -> a b", a=CHUNKS - 1)).then_inc(s_any, 16)
                sp.dma_start(dst_any[HEAD + PAD:], dst[HEAD:]).then_inc(s_any, 16)
                sp.wait_ge(s_f, 3)
                sp.dma_start(fields.rearrange("(p k) c -> p k c", p=SP_), field_f).then_inc(s_fs, 16)
                sp.wait_ge(s_pad, 1)
                at = HEAD
                while at < HEAD + PAD:
                    n = min(NT, HEAD + PAD - at)
                    sp.dma_start(dst_any[at:at + n].unsqueeze(0), pad[:, 0:n]).then_inc(s_any, 16)
                    at += n
                sp.wait_ge(s_any, 16 * (2 + -(-PAD // NT)))
                sp.wait_ge(s_x, 16 * (NB + 1))
                sp.wait_ge(s_fs, 16)

            @block.scalar
            def _(act):
                for n, (to, of) in enumerate([
                        (wm_top, W_msg[0:D, :]), (wm_bot, W_msg[D:, :]), (wu_top, W_upd[0:D, :]),
                        (wu_bot, W_upd[D:, :]), (w1_sb, W1), (w2_sb, W2)]):
                    act.dma_start(to[:, :], of).then_inc(s_w, 16)
                for to, of in ((bm_sb, b_msg), (bu_sb, b_upd), (gm_sb, gamma), (be_sb, beta), (b2_sb, b2), (b1_sb, b1)):
                    act.dma_start(to[:, :], of.partition_broadcast(P)).then_inc(s_w, 16)
                act.wait_ge(s_w, 16 * 12)

            @block.gpsimd
            def _(pool):
                pool.memset(ident[:, :], 0.0).then_inc(s_pc, 1)
                pool.iota(iota_i[:, :], pattern=[[1, P]], base=0, channel_multiplier=0)
                pool.iota(base_i[:, :], pattern=[[P, NT]], base=0, channel_multiplier=0)
                pool.iota(cell_i[:, :], pattern=[[1, CELLS]], base=1, channel_multiplier=0)
                pool.iota(window_i[:, :, :], pattern=[[SUB, WINDOWS], [0, WK]], base=0, channel_multiplier=0)\
                    .then_inc(s_pc, 1)
                pool.wait_ge(s_pc, 1)
                pool.affine_select(out=ident[:, :], in_=ident[:, :], compare_op=ALU.not_equal, fill=1.0, base=0,
                                   pattern=[[-1, P]], channel_multiplier=1).then_inc(s_pc, 1)
                pool.wait_ge(s_vc, 3)
                pool.memset(pad, -1).then_inc(s_pad, 1)

            @block.vector
            def _(dve):
                dve.memset(x_sb[:, FULL, :], 0.0).then_inc(s_vc, 1)
                dve.memset(ones[:, :], 1.0).then_inc(s_vc, 1)
                dve.memset(ones_b, 1.0)
                dve.memset(zero[:, :], 0.0)
                dve.memset(eps[:, :], EPS)
                dve.memset(neg_exact[:, :], -EXACT)
                dve.memset(zeros[:, :, :], 0.0)
                dve.memset(msgs[:, :, :, D:D + 1], 1.0)
                dve.wait_ge(s_pc, 3)
                dve.tensor_copy(iota[:, :], iota_i[:, :])
                dve.tensor_copy(iota_b[:, :], iota_i[:, :])
                dve.tensor_copy(cell_key[:, :], cell_i[:, :])
                dve.tensor_copy(window_base[:, :, :], window_i[:, :, :])
                dve.tensor_tensor(fold[:, :], ident[0:PARTS * HID, 0:HID], ident[0:PARTS * HID, HID:2 * HID], ALU.add)
                dve.tensor_scalar(window_no, cell_i[0:SP_, 0:NW], 1.0, None, ALU.subtract)
                dve.tensor_copy(node_base[:, :], base_i[:, :]).then_inc(s_vc, 1)
                dve.wait_ge(s_vc, 3)
                dve.tensor_tensor(fold[:, :], fold[:, :], ident[0:PARTS * HID, 2 * HID:3 * HID], ALU.add)
                dve.wait_ge(s_dst, 16)
                every = dst_i.rearrange("p (k s) -> p k s", s=STRIDE)[:, :, 0]
                dve.tensor_scalar(sample_i, every, 4, None, ALU.logical_shift_right).then_inc(s_vc, 1)
                assert SUB == 1 << 4
                dve.wait_ge(s_vc, 4)
                dve.tensor_copy(sample_f, sample_i).then_inc(s_vc, 1)
                dve.wait_ge(s_vc, 5)
                for n in range(SAMPLES // SB):
                    if n >= 2:
                        dve.wait_ge(s_sum, n - 1)
                    for j in range(SB):
                        last = dve.tensor_scalar(less[:, n % 2, j, :], window_no, sample_f[:, n * SB + j:n * SB + j + 1],
                                                 None, ALU.is_gt)
                    last.then_inc(s_less, 1)
                dve.wait_ge(s_src, 16)
                dve.tensor_copy(field_f[:, :, 0], dst_i).then_inc(s_f, 1)
                dve.tensor_scalar(high_i, src_i, 7, None, ALU.logical_shift_right).then_inc(s_vc, 1)
                dve.wait_ge(s_vc, 6)
                dve.tensor_scalar(field_f[:, :, 1], high_i, float(SUB), 1.0, ALU.mult, ALU.add).then_inc(s_f, 1)
                dve.wait_ge(s_f, 2)
                dve.tensor_scalar(high_i, src_i, P - 1, None, ALU.bitwise_and).then_inc(s_vc, 1)
                dve.wait_ge(s_vc, 7)
                dve.tensor_copy(field_f[:, :, 2], high_i).then_inc(s_f, 1)
                dve.wait_ge(s_sum, SAMPLES // SB)
                dve.tensor_scalar(starts_f[:, :], bank[0][0:1, 0:NW], float(STRIDE), float(-STRIDE), ALU.mult, ALU.add)\
                   .then_inc(s_vc, 1)
                dve.wait_ge(s_vc, 8)
                dve.tensor_scalar(starts[:, :], starts_f[:, :].rearrange("p (n w) -> p n w", w=WINDOWS)[:, :, 0],
                                  0.0, float(LAST_START), ALU.max, ALU.min)
                dve.tensor_scalar(window_starts[:, :], starts_f[:, :], 0.0, float(E - WEDGES), ALU.max, ALU.min)\
                   .then_inc(s_st, 1)

            @block.tensor
            def _(pe):
                pe.wait_ge(s_vc, 3)
                for n in range(SAMPLES // SB):
                    pe.wait_ge(s_less, n + 1)
                    for j in range(SB):
                        last = pe.matmul(bank[0][0:1, 0:NW], ones_b, less[:, n % 2, j, :],
                                         start=n + j == 0, stop=n * SB + j == SAMPLES - 1)
                    last.then_inc(s_sum, 1)
        clear(used)
        used.clear()

        s_v = sem("vector_steps_b")
        s_var = sem("variance_ready")
        s_std = sem("deviation_ready")
        s_tr = sem("transposes_done")
        s_ev = sem("transposes_copied")
        s_mm = sem("products_done")
        s_res = sem("result_ready")
        s_st = sem("result_stored")
        dense_sems = [s_v, s_var, s_std, s_tr, s_ev, s_mm, s_res, s_st]

        class Chain:
            def __init__(self, eng, s):
                self.eng, self.s, self.n = eng, s, 0

            def __call__(self, ins):
                self.n += 1
                ins.then_inc(self.s, 1)
                self.eng.wait_ge(self.s, self.n)

        def normalize(dve, step, of, to, scratch, nth):
            step(dve.tensor_reduce(stat[:, 0, :], of, AX.X, ALU.add))
            step(dve.tensor_scalar(stat[:, 1, :], stat[:, 0, :], -1.0 / D, None, ALU.mult))
            step(dve.tensor_tensor(to, of, wide(stat[:, 1, :]), ALU.add))
            step(dve.tensor_tensor(scratch, to, to, ALU.mult))
            step(dve.tensor_reduce(stat[:, 0, :], scratch, AX.X, ALU.add))
            dve.tensor_scalar(stat[:, 2, :], stat[:, 0, :], 1.0 / D, None, ALU.mult).then_inc(s_var, 1)
            dve.wait_ge(s_std, nth)
            step(dve.reciprocal(stat[:, 1, :], stat[:, 3, :]))
            step(dve.tensor_tensor(to, to, wide(stat[:, 1, :]), ALU.mult))

        def deviation(act, nth):
            act.wait_ge(s_var, nth)
            act.activation(stat[:, 3, :], stat[:, 2, :], ACT.Sqrt, bias=eps[:, 0:1]).then_inc(s_std, 1)

        def transpose_batch(pe, of, a, b):
            for t, place in enumerate(halves(a, b, BT)):
                last = pe.transpose(place, of[:, t, :], ident[:, :])
            return last

        def copy_batch(act, to, a, b):
            act.copy(to[:, 0:GT, :], block_of(a, GT))
            return act.copy(to[:, GT:BT, :], block_of(b, BT - GT))

        def add_banks(dve, step, to, a, b, row):
            dve.tensor_tensor(to[:, 0:GT, :], block_of(a, GT), over(row[:, :], GT), ALU.add)
            step(dve.tensor_tensor(to[:, GT:BT, :], block_of(b, BT - GT), over(row[:, :], BT - GT), ALU.add))

        with nc.Fori(0, NB) as i:
            tiles = bass.ds(i * BT, BT)
            with nc.Block() as block:
                @block.vector
                def _(dve):
                    step = Chain(dve, s_v)
                    normalize(dve, step, x_sb[:, tiles, :], bt0[:, :, :], bt1[:, :, :], 1)
                    step(dve.tensor_scalar(h_sb[:, tiles, :], bt0[:, :, :], 0.0, None, ALU.max))
                    dve.tensor_copy(bt0[:, :, :], h_sb[:, tiles, :]).then_inc(s_res, 1)
                    dve.wait_ge(s_mm, 1)
                    add_banks(dve, step, bt2, 2, 3, bm_sb)
                    dve.wait_ge(s_v, step.n)
                    dve.memset(stat[:, 0, 0:1], 0.0).then_inc(s_res, 1)

                @block.scalar
                def _(act):
                    deviation(act, 1)
                    act.wait_ge(s_tr, 1)
                    copy_batch(act, bt1, 0, 1).then_inc(s_ev, 1)

                @block.tensor
                def _(pe):
                    pe.wait_ge(s_res, 1)
                    transpose_batch(pe, bt0, 0, 1).then_inc(s_tr, 1)
                    pe.wait_ge(s_ev, 1)
                    for t, place in enumerate(halves(2, 3, BT)):
                        last = pe.matmul(place, bt1[:, t, :], wm_top[:, :], start=True, stop=True)
                    last.then_inc(s_mm, 1)

                @block.sync
                def _(sp):
                    sp.wait_ge(s_res, 2)
                    sp.dma_start(y_table[bass.ds(i * BT * P, BT * P), :].rearrange("(t p) f -> p t f", p=P),
                                 bt2[:, :, :]).then_inc(s_st, 16)
                    sp.wait_ge(s_st, 16)
            clear(dense_sems)

        g_names = ("rows_loaded", "edges_loaded", "rows_gathered",
                   "hot_ready", "edges_transposed", "edges_copied", "products", "messages", "scattered", "chunk_steps",
                   "summed")
        g = {n: sem("g_" + n) for n in g_names}

        def chunk_block(kind, table, start, dst_rows, node):
            width = D if kind == "message" else HID
            to = gathered[:, 0, :, 0:width] if kind == "message" else \
                gathered[:, 0, :, :].rearrange("p t f -> p (t f)")[:, 0:TILES * HID].rearrange("p (t f) -> p t f", f=HID)
            with nc.Block() as block:
                @block.sync
                def _(sp):
                    s = start(sp)
                    sp.dma_start(rows[:, 0, 0, :], src[bass.ds(s, CHUNK)].rearrange("(p j) -> p j", p=P))\
                      .then_inc(g["rows_loaded"], 16)
                    sp.dma_start(rows[:, 0, 1, :], dst_rows(s)).then_inc(g["rows_loaded"], 16)
                    if kind == "message":
                        sp.dma_start(edges[:, 0, :, :].rearrange("p j f -> p (j f)"),
                                     edge_attr[bass.ds(s, CHUNK), :].rearrange("(p j) f -> p (j f)", p=P))\
                          .then_inc(g["edges_loaded"], 16)

                @block.gpsimd
                def _(pool):
                    pool.wait_ge(g["rows_loaded"], 32)
                    for j in range(TILES):
                        pool.indirect_dma_start(to[:, j, :], None, table[:, :],
                                                bass.IndirectOffsetOnAxis(ap=rows[:, 0, 0, j:j + 1], axis=0))\
                            .then_inc(g["rows_gathered"], 16)
                    pool.wait_ge(g["rows_gathered"], 16 * TILES)

                @block.vector
                def _(dve):
                    step = Chain(dve, g["chunk_steps"])
                    dve.wait_ge(g["rows_loaded"], 32)
                    step(dve.tensor_tensor(dst_loc[:, 0, :], rows[:, 0, 1, :],
                                           node_base[:, bass.ds(node, 1)].to_broadcast([P, TILES]), ALU.subtract))
                    for n, (j, k) in enumerate(GROUPS):
                        if n:
                            dve.wait_ge(g["scattered"], n)
                        dve.tensor_tensor(hot[:, 0, 0:k, :], over(iota[:, :], k), wide(dst_loc[:, 0, j:j + k], P),
                                          ALU.is_equal).then_inc(g["hot_ready"], 1)
                        if n == 0:
                            dve.wait_ge(g["rows_gathered"], 16 * TILES)
                        if kind == "message":
                            dve.wait_ge(g["products"], n + 1)
                            pr = msgs[:, 1, 0:k, 0:D]
                            step(dve.tensor_tensor(pr, block_of(1, k), to[:, j:j + k, :], ALU.add))
                            dve.tensor_scalar(msgs[:, 0, 0:k, 0:D], pr, 0.0, None, ALU.max).then_inc(g["messages"], 1)
                    dve.wait_ge(g["scattered"], NG)
                    sums = agg if kind == "message" else conv
                    n = sums.shape[2]
                    dve.tensor_tensor(sums[:, bass.ds(node, 1), :].rearrange("p a f -> p (a f)"),
                                      sums[:, bass.ds(node, 1), :].rearrange("p a f -> p (a f)"),
                                      bank[4][:, 0:n], ALU.add).then_inc(g["summed"], 1)

                @block.scalar
                def _(act):
                    if kind == "message":
                        for n, (j, k) in enumerate(GROUPS):
                            act.wait_ge(g["edges_transposed"], n + 1)
                            act.copy(edges_T[:, 0, 0:k * P], bank[0][:, 0:k * P]).then_inc(g["edges_copied"], 1)

                @block.tensor
                def _(pe):
                    if kind == "message":
                        pe.wait_ge(g["edges_loaded"], 16)
                    else:
                        pe.wait_ge(g["rows_gathered"], 16 * TILES)
                    for n, (j, k) in enumerate(GROUPS):
                        if kind == "message":
                            for t in range(k):
                                last = pe.transpose(bank[0][:, t * P:t * P + P], edges[:, 0, j + t, :], ident[:, :])
                            last.then_inc(g["edges_transposed"], 1)
                            pe.wait_ge(g["edges_copied"], n + 1)
                            for t in range(k):
                                last = pe.matmul(bank[1][:, t * D:t * D + D], edges_T[:, 0, t * P:t * P + P],
                                                 wm_bot[:, :], start=True, stop=True)
                            last.then_inc(g["products"], 1)
                            pe.wait_ge(g["messages"], n + 1)
                        pe.wait_ge(g["hot_ready"], n + 1)
                        for t in range(k):
                            rhs = msgs[:, 0, t, :] if kind == "message" else to[:, j + t, :]
                            last = pe.matmul(bank[4][:, 0:rhs.shape[1]], hot[:, 0, t, :], rhs,
                                             start=j + t == 0, stop=j + t == TILES - 1)
                        last.then_inc(g["scattered"], 1)
            nc.gpsimd.dma_reset(range(g["rows_gathered"].num, g["rows_gathered"].num + 1))
            clear(list(g.values()))

        def pass_over_all(kind, table):
            with nc.Fori(0, NT) as i:
                with nc.Block() as block:
                    @block.vector
                    def _(dve):
                        sums = (agg if kind == "message" else conv)[:, bass.ds(i, 1), :]
                        dve.tensor_copy(sums, zeros[:, :, 0:sums.shape[2]])
                with nc.Fori(0, CHUNKS - 1) as c:
                    chunk_block(kind, table, lambda sp: c * CHUNK,
                                lambda s: dst_any[bass.ds(s, CHUNK)].rearrange("(p j) -> p j", p=P), i)
                chunk_block(kind, table, lambda sp: LAST_START,
                            lambda s: dst_any[HEAD:HEAD + CHUNK].rearrange("(p j) -> p j", p=P), i)

        def in_sem(name):
            return [sem(f"{name}{q}") for q in range(2)]

        rows_in, keys_in, edges_in = in_sem("rows_in"), in_sem("keys_in"), in_sem("edges_in")
        group_in = [[sem(f"group{n}_in{q}") for n in range(NG)] for q in range(2)]
        cells_stored = sem("cells_stored")
        (transposed, copied, products, added, msgs_ready, hot_ready, scattered, agg_copied, cell_hots, half_done,
         half_copied, columns) = (sem("m_" + n) for n in (
             "transposed", "copied", "products", "added", "msgs_ready", "hot_ready", "scattered", "agg_copied",
             "cell_hots", "half_done", "half_copied", "columns"))
        tp, pm, acc, cell_bank = bank[0:2], bank[2:4], bank[4], bank[5:7]
        COLUMNS = 8
        H = len(HALVES)

        stood = sem("stood")

        def at_least(eng, s, v):
            if not isinstance(v, int) or v > 0:
                eng.wait_ge(s, v)

        def over_chunks(eng, emit):
            emit(0, 0, 0, True)
            emit(1, 1, 0, True)
            with eng.Fori(1, NT // 2) as i:
                emit(i * 2, 0, i, True)
                emit(i * 2 + 1, 1, i, True)
            emit(NT - 1, 0, NT // 2, False)

        with nc.Block() as block:
            @block.sync
            def _(sp):
                def load(k, q):
                    s = sp.value_load(starts[0:1, bass.ds(k, 1)], min_val=0, max_val=LAST_START)
                    sp.dma_start(rows[:, q, 0, :], src[bass.ds(s, CHUNK)].rearrange("(p j) -> p j", p=P))\
                      .then_inc(rows_in[q], 16)
                    sp.dma_start(rows[:, q, 1, :], dst[bass.ds(s, CHUNK)].rearrange("(p j) -> p j", p=P))\
                      .then_inc(rows_in[q], 16)
                    sp.dma_start(edges[:, q, :, :].rearrange("p j f -> p (j f)"),
                                 edge_attr[bass.ds(s, CHUNK), :].rearrange("(p j) f -> p (j f)", p=P))\
                      .then_inc(edges_in[q], 16)
                    for w in range(WINDOWS):
                        s = sp.value_load(window_starts[0:1, bass.ds(k * WINDOWS + w, 1)], min_val=0,
                                          max_val=E - WEDGES)
                        sp.dma_start(keys[:, q, w, :, :].rearrange("p j c -> p (j c)"),
                                     fields[bass.ds(s, WEDGES), :].rearrange("(p j) c -> p (j c)", p=P))\
                          .then_inc(keys_in[q], 16)

                def emit(k, q, i, more):
                    if more:
                        at_least(sp, added, k * NG)
                        at_least(sp, transposed, k * NG)
                        sp.sem_inc(stood, 1)
                        at_least(sp, cell_hots, k * WINDOWS)
                        sp.sem_inc(stood, 1)
                        load(k + 1, 1 - q)
                    at_least(sp, half_copied, k * WINDOWS * H + WINDOWS * H)
                    sp.sem_inc(stood, 1)
                    sp.dma_start(adjacency[bass.ds(k, 1), :, :].rearrange("a p n -> (a p) n"), cells[:, :].bitcast(U8))\
                      .then_inc(cells_stored, 16)

                load(0, 0)
                over_chunks(sp, emit)
                sp.wait_ge(cells_stored, 16 * NT)

            @block.gpsimd
            def _(pool):
                def emit(k, q, i, more):
                    at_least(pool, rows_in[q], i * 32 + 32)
                    at_least(pool, added, k * NG - NG)
                    pool.sem_inc(stood, 1)
                    for n, (j, c) in enumerate(GROUPS):
                        for t in range(j, j + c):
                            pool.indirect_dma_start(gathered[:, q, t, :], None, y_table[:, :],
                                                    bass.IndirectOffsetOnAxis(ap=rows[:, q, 0, t:t + 1], axis=0))\
                                .then_inc(group_in[q][n], 16)

                over_chunks(pool, emit)

            @block.vector
            def _(dve):
                def emit(k, q, i, more):
                    done = [0]

                    def column(ins, wait=True):
                        done[0] += 1
                        ins.then_inc(columns, 1)
                        if wait:
                            dve.wait_ge(columns, k * COLUMNS + done[0])

                    base = node_base[:, bass.ds(k, 1)]
                    at_least(dve, rows_in[q], i * 32 + 32)
                    column(dve.tensor_scalar(dst_loc[:, q, :], rows[:, q, 1, :], base, None, ALU.subtract), False)
                    at_least(dve, keys_in[q], i * 16 * WINDOWS + 16 * WINDOWS)
                    d, inside = key_tmp[:, 0, :, :], key_tmp[:, 1, :, :]
                    column(dve.tensor_scalar(d, keys[:, q, :, :, 0], base, None, ALU.subtract))
                    column(dve.tensor_tensor(d, d, window_base[:, :, :], ALU.subtract))
                    column(dve.tensor_scalar(inside, d, 0.0, None, ALU.is_ge))
                    column(dve.scalar_tensor_tensor(inside, d, float(SUB), inside, ALU.is_lt, ALU.mult))
                    column(dve.tensor_tensor(d, d, keys[:, q, :, :, 1], ALU.add))
                    column(dve.tensor_tensor(cell_of[:, q, :, :], d, inside, ALU.mult), False)
                    column(dve.tensor_copy(src_low[:, q, :, :], keys[:, q, :, :, 2]))
                    assert done[0] == COLUMNS
                    for n, (j, c) in enumerate(GROUPS):
                        b = (q * NG + n) % 2
                        at_least(dve, scattered, k * NG + (n - 1))
                        dve.tensor_tensor(hot[:, b, 0:c, :], over(iota[:, :], c), wide(dst_loc[:, q, j:j + c], P),
                                          ALU.is_equal).then_inc(hot_ready, 1)
                        if n < WINDOWS:
                            at_least(dve, half_done, k * WINDOWS * H + (n - 1) * H)
                            for t in range(WK):
                                dve.tensor_scalar(cell_hot[:, n % 2, t, :], cell_key[:, :], cell_of[:, q, n, t:t + 1],
                                                  None, ALU.is_equal)
                            dve.tensor_tensor(low_hot[:, n % 2, :, :], over(iota_b[:, :], WK),
                                              wide(src_low[:, q, n, :], P), ALU.is_equal).then_inc(cell_hots, 1)
                        if n == 0 and not (isinstance(k, int) and k == 0):
                            copy_sums(k - 1, k * NG)
                        dve.wait_ge(products, k * NG + (n + 1))
                        dve.wait_ge(group_in[q][n], i * 16 * c + 16 * c)
                        dve.tensor_tensor(msgs[:, b, 0:c, 0:D],
                                          pm[b][:, 0:c * D].rearrange("p (t f) -> p t f", f=D),
                                          gathered[:, q, j:j + c, :], ALU.add).then_inc(added, 1)

                def copy_sums(k, groups):
                    dve.wait_ge(scattered, groups)
                    dve.tensor_copy(agg[:, bass.ds(k, 1), :].rearrange("p a f -> p (a f)"), acc[:, 0:D + 1])\
                       .then_inc(agg_copied, 1)

                over_chunks(dve, emit)
                copy_sums(NT - 1, NT * NG)

            @block.scalar
            def _(act):
                def emit(k, q, i, more):
                    for n, (j, c) in enumerate(GROUPS):
                        b = (q * NG + n) % 2
                        act.wait_ge(transposed, k * NG + (n + 1))
                        at_least(act, products, k * NG + (n - 1))
                        act.copy(edges_T[:, b, 0:c * P], tp[b][:, 0:c * P]).then_inc(copied, 1)
                        if 1 <= n <= WINDOWS:
                            window(k, q, i, n - 1)
                        act.wait_ge(added, k * NG + (n + 1))
                        act.activation(msgs[:, b, 0:c, 0:D], msgs[:, b, 0:c, 0:D], ACT.Relu).then_inc(msgs_ready, 1)
                    act.wait_ge(half_copied, k * WINDOWS * H + WINDOWS * H)
                    act.copy(tallies[:, :, bass.ds(k, 1), :].rearrange("p c k n -> p c (k n)"), tally[:, q, :, :])

                def window(k, q, i, w):
                    for h, (lo, hi) in enumerate(HALVES):
                        act.wait_ge(half_done, k * WINDOWS * H + (w * H + h + 1))
                        if w + h == 0:
                            at_least(act, cells_stored, k * 16)
                        act.sem_inc(stood, 1)
                        col = w * H + h
                        act.activation(cells[:, w * CELLS + lo:w * CELLS + hi], cell_bank[h][:, 0:hi - lo],
                                       ACT.Copy, accum_out=tally[:, q, 0, col:col + 1], saturate=False)
                        at_least(act, half_copied, k * WINDOWS * H + (w * H + h - 1))
                        act.activation(over_junk[:, h, 0:hi - lo], cell_bank[h][:, 0:hi - lo], ACT.Relu,
                                       bias=neg_exact[:, 0:1], accum_out=tally[:, q, 1, col:col + 1]).then_inc(half_copied, 1)

                over_chunks(act, emit)

            @block.tensor
            def _(pe):
                def emit(k, q, i, more):
                    for n in range(NG + 1):
                        b = (q * NG + n) % 2
                        if n < NG:
                            j, c = GROUPS[n]
                            if n == 0:
                                pe.wait_ge(edges_in[q], i * 16 + 16)
                            at_least(pe, copied, k * NG + (n - 1))
                            for t in range(c):
                                last = pe.transpose(tp[b][:, t * P:t * P + P], edges[:, q, j + t, :], ident[:, :])
                            last.then_inc(transposed, 1)
                        if 1 <= n <= WINDOWS:
                            half(k, n - 1, 0)
                        if n < NG:
                            pe.wait_ge(copied, k * NG + (n + 1))
                            at_least(pe, added, k * NG + (n - 1))
                            for t in range(c):
                                last = pe.matmul(pm[b][:, t * D:t * D + D], edges_T[:, b, t * P:t * P + P],
                                                 wm_bot[:, :], start=True, stop=True)
                            last.then_inc(products, 1)
                        if 1 <= n <= WINDOWS:
                            half(k, n - 1, 1)
                        if n >= 1:
                            j, c = GROUPS[n - 1]
                            pe.wait_ge(msgs_ready, k * NG + n)
                            pe.wait_ge(hot_ready, k * NG + n)
                            if n == 1:
                                at_least(pe, agg_copied, k)
                            for t in range(c):
                                last = pe.matmul(acc[:, 0:D + 1], hot[:, 1 - b, t, :], msgs[:, 1 - b, t, :],
                                                 start=j + t == 0, stop=j + t == TILES - 1)
                            last.then_inc(scattered, 1)

                def half(k, w, h):
                    lo, hi = HALVES[h]
                    if h == 0:
                        pe.wait_ge(cell_hots, k * WINDOWS + (w + 1))
                    at_least(pe, half_copied, k * WINDOWS * H + (w * H + h - 1))
                    for t in range(WK):
                        last = pe.matmul(cell_bank[h][:, 0:hi - lo], low_hot[:, w % 2, t, :],
                                         cell_hot[:, w % 2, t, lo:hi], start=t == 0, stop=t == WK - 1)
                    last.then_inc(half_done, 1)

                over_chunks(pe, emit)

        s_c, s_m, s_ms = sem("miss_columns"), sem("miss_summed"), sem("miss_set")
        with nc.Block() as block:
            @block.vector
            def _(dve):
                dve.tensor_reduce(miss_col[:, 0:1], agg[:, :, D:D + 1].rearrange("p n a -> p (n a)"), AX.X, ALU.add)
                dve.tensor_reduce(miss_col[:, 1:2], tallies[:, 0, :, :].rearrange("p k n -> p (k n)"), AX.X, ALU.add)
                dve.tensor_reduce(miss_col[:, 2:3], tallies[:, 1, :, :].rearrange("p k n -> p (k n)"), AX.X, ALU.add).then_inc(s_c, 1)
                dve.wait_ge(s_m, 1)
                dve.tensor_scalar(miss[:, :], bank[0][0:1, 0:2], -1.0, float(E), ALU.mult, ALU.add).then_inc(s_ms, 1)
                dve.wait_ge(s_ms, 1)
                dve.tensor_tensor(miss[:, 1:2], miss[:, 1:2], bank[0][0:1, 2:3], ALU.add).then_inc(s_ms, 1)
                dve.wait_ge(s_ms, 2)

            @block.tensor
            def _(pe):
                pe.wait_ge(s_c, 1)
                pe.matmul(bank[0][0:1, 0:3], ones[:, :], miss_col[:, :], start=True, stop=True).then_inc(s_m, 1)
        missed = nc.values_load(miss[0:1, 0:1], min_val=0, max_val=E)
        inexact = nc.values_load(miss[0:1, 1:2], min_val=0, max_val=2 * E)
        with nc.If(missed != 0):
            pass_over_all("message", y_table)

        with nc.Fori(0, NB) as i:
            tiles = bass.ds(i * BT, BT)
            counts = agg[:, tiles, D:D + 1].rearrange("p n a -> p (n a)")
            with nc.Block() as block:
                @block.vector
                def _(dve):
                    step = Chain(dve, s_v)
                    step(dve.tensor_scalar(stat[:, 0, :], counts, 1.0, None, ALU.max))
                    step(dve.reciprocal(stat[:, 1, :], stat[:, 0, :]))
                    step(dve.tensor_tensor(bt0[:, :, :], agg[:, tiles, 0:D], wide(stat[:, 1, :]), ALU.mult))
                    dve.tensor_copy(bt1[:, :, :], h_sb[:, tiles, :]).then_inc(s_res, 1)
                    dve.wait_ge(s_mm, 1)
                    add_banks(dve, step, bt0, 4, 5, bu_sb)
                    normalize(dve, step, bt0[:, :, :], bt1[:, :, :], bt2[:, :, :], 1)
                    step(dve.tensor_tensor(bt1[:, :, :], bt1[:, :, :], over(gm_sb[:, :], BT), ALU.mult))
                    step(dve.tensor_tensor(bt1[:, :, :], bt1[:, :, :], over(be_sb[:, :], BT), ALU.add))
                    step(dve.tensor_tensor(bt1[:, :, :], bt1[:, :, :], h_sb[:, tiles, :], ALU.add))
                    step(dve.tensor_scalar(bt1[:, :, :], bt1[:, :, :], 0.0, None, ALU.max))
                    step(dve.tensor_tensor(x_sb[:, tiles, :], x_sb[:, tiles, :], bt1[:, :, :], ALU.add))
                    normalize(dve, step, x_sb[:, tiles, :], bt0[:, :, :], bt2[:, :, :], 2)
                    step(dve.tensor_scalar(stat[:, 2, :], counts, 1.0, None, ALU.add))
                    dve.tensor_scalar(bt0[:, :, :], bt0[:, :, :], 0.0, None, ALU.max).then_inc(s_res, 1)
                    dve.wait_ge(s_std, 3)
                    step(dve.reciprocal(dinv[:, tiles], stat[:, 3, :]))
                    dve.wait_ge(s_mm, 2)
                    step(dve.tensor_tensor(z_sb[:, tiles, :], block_of(6, BT, HID), wide(dinv[:, tiles], HID), ALU.mult))

                @block.scalar
                def _(act):
                    act.wait_ge(s_tr, 1)
                    copy_batch(act, bt2, 0, 1)
                    copy_batch(act, bt3, 2, 3).then_inc(s_ev, 1)
                    deviation(act, 1)
                    deviation(act, 2)
                    act.wait_ge(s_res, 2)
                    act.activation(stat[:, 3, :], stat[:, 2, :], ACT.Sqrt, bias=zero[:, 0:1]).then_inc(s_std, 1)
                    act.wait_ge(s_tr, 2)
                    copy_batch(act, bt1, 0, 1).then_inc(s_ev, 1)

                @block.tensor
                def _(pe):
                    pe.wait_ge(s_res, 1)
                    transpose_batch(pe, bt0, 0, 1)
                    transpose_batch(pe, bt1, 2, 3).then_inc(s_tr, 1)
                    pe.wait_ge(s_ev, 1)
                    for t, place in enumerate(halves(4, 5, BT)):
                        pe.matmul(place, bt3[:, t, :], wu_top[:, :], start=True, stop=False)
                        last = pe.matmul(place, bt2[:, t, :], wu_bot[:, :], start=False, stop=True)
                    last.then_inc(s_mm, 1)
                    pe.wait_ge(s_res, 2)
                    transpose_batch(pe, bt0, 0, 1).then_inc(s_tr, 1)
                    pe.wait_ge(s_ev, 2)
                    for t in range(BT):
                        last = pe.matmul(bank[6][:, t * HID:(t + 1) * HID], bt1[:, t, :], w1_sb[:, :],
                                         start=True, stop=True)
                    last.then_inc(s_mm, 1)
            clear(dense_sems)

        def table_rows(table):
            return table[:, :].rearrange("(t p) f -> p t f", p=P)

        quad_in = in_sem("quad_in")
        split_done, quad_done, quad_copied, folded, fold_copied = (
            sem("c_" + n) for n in ("split_done", "quad_done", "quad_copied", "folded", "fold_copied"))
        conv_sems = [*quad_in, split_done, quad_done, quad_copied, folded, fold_copied]
        QUAD = QT * WINDOWS * CELLS
        slots = work[:, :, :].rearrange("p q n -> p (q n)").bitcast(FP8)[:, 0:2 * QUAD].rearrange("p (q n) -> p q n", q=2)
        assert QUADS % 2 == 0 and 0 < NT % QT
        rest = NT % QT

        def split(dve):
            z, r = z_sb[:, :, :], conv[:, :, :]
            step = Chain(dve, s_v)
            step(dve.tensor_copy(parts[:, :, 0, :], z))
            step(dve.tensor_tensor(r, z, parts[:, :, 0, :], ALU.subtract))
            step(dve.tensor_copy(parts[:, :, 1, :], r))
            step(dve.tensor_tensor(r, r, parts[:, :, 1, :], ALU.subtract))
            dve.tensor_copy(parts[:, :, 2, :], r).then_inc(split_done, 1)
            dve.wait_ge(split_done, 1)

        def convolve_dense():
            def over_quads(eng, emit):
                emit(0, 0, 0, QT)
                emit(1, 1, 0, QT)
                if QUADS > 2:
                    with eng.Fori(1, QUADS // 2) as i:
                        emit(i * 2, 0, i, QT)
                        emit(i * 2 + 1, 1, i, QT)
                emit(QUADS, 0, QUADS // 2, rest)

            with nc.Block() as block:
                @block.sync
                def _(sp):
                    def emit(n, q, i, tiles):
                        at_least(sp, quad_done, n - 1)
                        sp.sem_inc(stood, 1)
                        sp.dma_start(slots[:, q, 0:tiles * WINDOWS * CELLS].bitcast(U8)
                                     .rearrange("p (t n) -> p t n", t=tiles),
                                     adjacency[bass.ds(n * QT, tiles), :, :].rearrange("t p n -> p t n"))\
                          .then_inc(quad_in[q], 16)
                    over_quads(sp, emit)

                @block.tensor
                def _(pe):
                    def emit(n, q, i, tiles):
                        pe.wait_ge(quad_in[q], i * 16 + 16)
                        at_least(pe, quad_copied, n - 1)
                        pe.sem_inc(stood, 1)
                        cell = slots[:, q, 0:tiles * WINDOWS * CELLS].rearrange("p (w a d) -> p w a d", a=NT, d=SUB)
                        for a in range(NT):
                            last = pe.matmul(bank[q][0:PARTS * HID, 0:tiles * P],
                                             parts[:, a, :, :].rearrange("p c f -> p (c f)"), cell[:, :, a, :],
                                             start=a == 0, stop=a == NT - 1)
                        last.then_inc(quad_done, 1)
                        if not (isinstance(n, int) and n == 0):
                            fold_quad(n - 1, 1 - q, QT)

                    def fold_quad(n, q, tiles):
                        pe.wait_ge(quad_copied, n + 1)
                        at_least(pe, fold_copied, n - 1)
                        for t in range(tiles):
                            last = pe.matmul(bank[2 + q][:, t * HID:(t + 1) * HID], part_sums[:, q, t * P:(t + 1) * P],
                                             fold[:, :], start=True, stop=True)
                        last.then_inc(folded, 1)

                    pe.wait_ge(split_done, 1)
                    over_quads(pe, emit)
                    fold_quad(QUADS, 0, rest)

                @block.scalar
                def _(act):
                    def emit(n, q, i, tiles):
                        act.wait_ge(quad_done, n + 1)
                        at_least(act, folded, n - 1)
                        act.copy(part_sums[:, q, 0:tiles * P], bank[q][0:PARTS * HID, 0:tiles * P])\
                           .then_inc(quad_copied, 1)
                    over_quads(act, emit)

                @block.vector
                def _(dve):
                    split(dve)

                    def emit(n, q, i, tiles):
                        dve.wait_ge(folded, n + 1)
                        dve.tensor_copy(conv[:, bass.ds(n * QT, tiles), :], block_of(2 + q, tiles, HID))\
                           .then_inc(fold_copied, 1)
                    over_quads(dve, emit)
            clear([*conv_sems, s_v])

        def convolve(table):
            convolve_dense()
            with nc.If(inexact != 0):
                with nc.Fori(0, 1) as once:
                    with nc.Block() as block:
                        @block.sync
                        def _(sp):
                            sp.dma_start(table_rows(table), z_sb[:, :, :]).then_inc(s_st, 16)
                            sp.wait_ge(s_st, 16)
                    clear([s_st])
                pass_over_all("row", table)

        convolve(z1_table)
        with nc.Block() as block:
            @block.vector
            def _(dve):
                step = Chain(dve, s_v)
                step(dve.tensor_tensor(conv[:, :, :], conv[:, :, :], z_sb[:, :, :], ALU.add))
                step(dve.tensor_tensor(conv[:, :, :], conv[:, :, :], wide(dinv[:, :], HID), ALU.mult))
                step(dve.tensor_tensor(conv[:, :, :], conv[:, :, :], over(b1_sb[:, :], NT), ALU.add))
                step(dve.tensor_scalar(conv[:, :, :], conv[:, :, :], 0.0, None, ALU.max))
                step(dve.tensor_tensor(z_sb[:, :, :], conv[:, :, :], wide(dinv[:, :], HID), ALU.mult))
        clear(dense_sems)

        convolve(z2_table)
        with nc.Block() as block:
            @block.vector
            def _(dve):
                step = Chain(dve, s_v)
                step(dve.tensor_tensor(conv[:, :, :], conv[:, :, :], z_sb[:, :, :], ALU.add))
                step(dve.tensor_tensor(conv[:, :, :], conv[:, :, :], wide(dinv[:, :], HID), ALU.mult))
        clear(dense_sems)
        with nc.Fori(0, NB) as i:
            tiles = bass.ds(i * BT, BT)
            with nc.Block() as block:
                @block.vector
                def _(dve):
                    dve.tensor_copy(bt0[:, :, 0:HID], conv[:, tiles, :]).then_inc(s_res, 1)
                    dve.wait_ge(s_mm, 1)
                    step = Chain(dve, s_v)
                    add_banks(dve, step, bt2, 2, 3, b2_sb)
                    step(dve.tensor_tensor(x_sb[:, tiles, :], x_sb[:, tiles, :], bt2[:, :, :], ALU.add))

                @block.tensor
                def _(pe):
                    pe.wait_ge(s_res, 1)
                    for t, place in enumerate(halves(0, 1, BT)):
                        last = pe.transpose(place[0:HID, :], bt0[:, t, 0:HID], ident[:, :])
                    last.then_inc(s_tr, 1)
                    pe.wait_ge(s_ev, 1)
                    for t, place in enumerate(halves(2, 3, BT)):
                        last = pe.matmul(place, bt1[0:HID, t, :], w2_sb[:, :], start=True, stop=True)
                    last.then_inc(s_mm, 1)

                @block.scalar
                def _(act):
                    act.wait_ge(s_tr, 1)
                    act.copy(bt1[0:HID, 0:GT, :], block_of(0, GT)[0:HID])
                    act.copy(bt1[0:HID, GT:BT, :], block_of(1, BT - GT)[0:HID]).then_inc(s_ev, 1)
            clear(dense_sems)
        with nc.Block() as block:
            @block.sync
            def _(sp):
                sp.dma_start(out[0:FULL * P, :].rearrange("(t p) f -> p t f", p=P), x_sb[:, 0:FULL, :])\
                  .then_inc(s_st, 16)
                sp.dma_start(out[FULL * P:N, :], x_sb[0:TAIL, FULL, :]).then_inc(s_st, 16)
                sp.wait_ge(s_st, 32)


_INS = ["x", "src", "dst", "edge_attr_128", "L0_gnn_W_msg", "L0_gnn_b_msg", "L0_gnn_W_upd", "L0_gnn_b_upd",
        "L0_gnn_gamma", "L0_gnn_beta", "L1_gnn_W1", "L1_gnn_b1", "L1_gnn_W2", "L1_gnn_b2"]


def kernel(**inputs):
    import numpy as _np
    import concourse.bacc as _bacc
    from concourse import mybir as _mybir
    from concourse.bass_utils import run_bass_kernel_spmd as _run

    nc = _bacc.Bacc("TRN2", target_bir_lowering=False, num_devices=1)
    arrays, args = {}, []
    for name in _INS:
        a = _np.ascontiguousarray(inputs[name])
        arrays[f"in_{name}"] = a
        args.append(nc.dram_tensor(f"in_{name}", a.shape, _mybir.dt.from_np(a.dtype), kind="ExternalInput").ap())
    args.append(nc.dram_tensor("out_nodes", arrays["in_x"].shape, _mybir.dt.float32, kind="ExternalOutput").ap())
    gnn_kernel(nc, *args)
    r = _run(nc, [arrays], core_ids=[0])
    return r.results[0]["out_nodes"]
```

```python
import concourse.bass as bass
from concourse import mybir
from contextlib import ExitStack

F32 = mybir.dt.float32
I32 = mybir.dt.int32
F16 = mybir.dt.float16
BF16 = mybir.dt.bfloat16
FP8 = mybir.dt.float8e4
U8 = mybir.dt.uint8
ALU = mybir.AluOpType
ACT = mybir.ActivationFunctionType
AX = mybir.AxisListType
P = 128
EPS = 1e-5


def gnn_kernel(nc, x, src, dst, edge_attr, W_msg, b_msg, W_upd, b_upd, gamma, beta, W1, b1, W2, b2, out):
    N, D = x.shape
    E = src.shape[0]
    HID = W1.shape[1]
    NT = -(-N // P)
    FULL = N // P
    TAIL = N - FULL * P
    TILES = -(-E // N) + 2
    CHUNK = TILES * P
    GT = 512 // D
    GROUPS = [(g, min(GT, TILES - g)) for g in range(0, TILES, GT)]
    NG = len(GROUPS)
    LAST_START = E - CHUNK
    CHUNKS = -(-E // CHUNK)
    BT = 7 if NT % 7 == 0 else 5
    NB = NT // BT
    assert NT % BT == 0 and NT % 2 == 1 and NB >= 5
    SUB = 16
    WINDOWS = P // SUB
    WK = -(-(SUB * E // N) // P) + 1
    WEDGES = WK * P
    CELLS = NT * SUB
    HALVES = [(0, (NT + 1) // 2 * SUB), ((NT + 1) // 2 * SUB, CELLS)]
    COUNTS = NT * P
    EXACT = 16.0
    PARTS = 3
    FIELDS = 3
    QT = 4
    QUADS = NT // QT
    RING = 3
    ROUNDS = QUADS // RING
    SP_ = 125
    STRIDE = 32
    PER = E // SP_
    assert PER % STRIDE == 0 and D == P

    ctx = ExitStack()
    with ctx:
        def sb(name, shape, dt=F32):
            return ctx.enter_context(nc.sbuf_tensor(name, shape, dt))

        def sem(name):
            return ctx.enter_context(nc.semaphore(name))

        def clear(sems):
            for s in sems:
                nc.sync.sem_clear(s)
            nc.all_engine_barrier()

        y_table = nc.dram_tensor("y_table", [NT * P, D], F32)
        z_table = nc.dram_tensor("z_table", [NT * P, HID], F32)
        adjacency = nc.dram_tensor("adjacency", [NT, P, COUNTS], U8)
        fields = nc.dram_tensor("fields", [E, FIELDS], F32)
        dst_any = nc.dram_tensor("dst_any", [CHUNKS * CHUNK], I32)

        x_sb = sb("x_sb", [P, NT, D])
        h_sb = sb("h_sb", [P, NT, D])
        agg = sb("agg", [P, NT, D + 1])
        conv = sb("conv", [P, NT, HID])
        z_sb = sb("z_sb", [P, NT, HID])
        dinv = sb("dinv", [P, NT])
        work = sb("work", [P, 4, TILES * D])
        by_parity = work[:, :, :].rearrange("p (q s) (t f) -> p q s t f", s=2, f=D)
        edges, gathered = by_parity[:, :, 0, :, :], by_parity[:, :, 1, :, :]
        ident = sb("ident", [P, P])
        iota_i = z_sb[:, :, :].rearrange("p n f -> p (n f)").bitcast(I32)[:, 0:P]
        iota = sb("iota", [P, P])
        base_i = sb("base_i", [P, NT], I32)
        node_base = sb("node_base", [P, NT])
        ones = sb("ones", [P, 1])
        zero = sb("zero", [P, 1])
        zeros = sb("zeros", [P, 1, D + 1])
        eps = sb("eps", [P, 1])
        wm_top, wm_bot = sb("wm_top", [P, D]), sb("wm_bot", [P, D])
        wu_top, wu_bot = sb("wu_top", [P, D]), sb("wu_bot", [P, D])
        w1_sb, w2_sb = sb("w1_sb", [P, HID]), sb("w2_sb", [HID, D])
        bm_sb, bu_sb, gm_sb, be_sb, b2_sb = (sb(n, [P, D]) for n in ("bm_sb", "bu_sb", "gm_sb", "be_sb", "b2_sb"))
        b1_sb = sb("b1_sb", [P, HID])
        starts_f = sb("starts_f", [1, NT * WINDOWS])
        window_starts = sb("window_starts", [1, NT * WINDOWS], I32)
        starts = sb("starts", [1, NT], I32)
        miss = sb("miss", [1, 2], I32)
        miss_col = sb("miss_col", [P, 3])
        rows = sb("rows", [P, 2, 2, TILES], I32)
        keys = sb("keys", [P, 2, WINDOWS, WK, FIELDS])
        window_base = sb("window_base", [P, WINDOWS, WK])
        window_i = sb("window_i", [P, WINDOWS, WK], I32)
        cell_i = conv[:, :, :].rearrange("p n f -> p (n f)").bitcast(I32)[:, 0:CELLS]
        cell_key = sb("cell_key", [P, CELLS], F16)
        iota_b = sb("iota_b", [P, P], BF16)
        key_tmp = sb("key_tmp", [P, 2, WINDOWS, WK])
        cell_of = sb("cell_of", [P, 2, WINDOWS, WK])
        src_low = sb("src_low", [P, 2, WINDOWS, WK], BF16)
        cell_hot = sb("cell_hot", [P, 2, WK, CELLS], BF16)
        low_hot = sb("low_hot", [P, 2, WK, P], BF16)
        cells = sb("cells", [P, NT, WINDOWS, SUB], FP8)
        over_junk = sb("over_junk", [P, 2, HALVES[0][1]], BF16)
        assert HID >= SUB
        tally = sb("tally", [P, 2, 2, 2 * WINDOWS])
        tallies = sb("tallies", [P, 2, 2 * WINDOWS])
        neg_exact = sb("neg_exact", [P, 1])
        parts = h_sb[:, :, :].rearrange("p n f -> p (n f)").bitcast(BF16)[:, 0:2 * NT * PARTS * HID]\
            .rearrange("p (v n c f) -> p v n c f", v=2, c=PARTS, f=HID)
        parts = [parts[:, v, :, :, :] for v in range(2)]
        dst_loc = sb("dst_loc", [P, 2, TILES])
        edges_T = sb("edges_T", [P, 2, 512])
        msgs = sb("msgs", [P, 2, GT, D + 1])
        hot = sb("hot", [P, 2, GT, P])
        u_sb, mean_sb, h_now, h2_sb, h2t_sb = (sb(n, [P, D]) for n in ("u_sb", "mean_sb", "h_now", "h2_sb", "h2t_sb"))
        tu_sb = sb("tu_sb", [P, 2 * D])
        ut, ust, uag = sb("ut", [P, 12]), sb("ust", [P, 12]), sb("uag", [P, 4])
        stat = sb("stat", [P, 4, BT])
        stats, moments = sb("stats", [P, 2, BT, 6]), sb("moments", [P, 2, BT, 2])
        roots, scales, shifts = (sb(n, [P, 2, BT]) for n in ("roots", "scales", "shifts"))
        bt0, bt1, bt2, bt3 = (work[:, 1, i * BT * D:(i + 1) * BT * D].rearrange("p (t f) -> p t f", f=D)
                              for i in range(4))

        bank = [ctx.enter_context(nc.psum_tensor(f"bank{i}", [P, 512], F32)) for i in range(8)]

        def wide(ap, n=D):
            return ap.unsqueeze(2).to_broadcast([ap.shape[0], ap.shape[1], n])

        def over(ap, k):
            return ap.unsqueeze(1).to_broadcast([ap.shape[0], k, ap.shape[1]])

        def halves(a, b, n, w=D):
            per = 512 // D
            return [(bank[(a, b)[t // per]][:, (t % per) * w:(t % per) * w + w]) for t in range(n)]

        def block_of(a, k, w=D):
            return bank[a][:, 0:k * w].rearrange("p (t f) -> p t f", f=w)

        def column_of(tensor, m):
            return tensor[:, bass.ds(m, 1), :].rearrange("p a f -> p (a f)")

        stood = sem("stood")

        def at_least(eng, s, v):
            if not isinstance(v, int) or v > 0:
                eng.wait_ge(s, v)

        def is_first(k, n):
            return isinstance(k, int) and k < n

        def over_batches(eng, emit):
            for b in range(4):
                emit(b, b % 2)
            if NB > 5:
                with eng.Fori(2, NB // 2) as i:
                    emit(i * 2, 0)
                    emit(i * 2 + 1, 1)
            emit(NB - 1, 0)

        s_x, s_w, s_dst, s_pad, s_any = (sem(n) for n in ("x_loaded", "weights_loaded", "dst_loaded", "pad_set",
                                                         "dst_any_written"))
        s_pc, s_vc, s_st = (sem(n) for n in ("pool_consts", "vector_steps", "starts_set"))
        room = work[0:SP_, :, :].rearrange("p q n -> p (q n)")
        src_i = room[:, 0:PER].bitcast(I32)
        dst_i = room[:, PER:2 * PER].bitcast(I32)
        field_f = room[:, 2 * PER:(2 + FIELDS) * PER].rearrange("p (k c) -> p k c", c=FIELDS)
        high_i = room[:, (2 + FIELDS) * PER:(3 + FIELDS) * PER].bitcast(I32)
        low_i = room[:, (3 + FIELDS) * PER:(4 + FIELDS) * PER].bitcast(I32)
        free = (4 + FIELDS) * PER
        h_now_b = work[:, :, :].rearrange("p q n -> p (q n)")[:, free:free + 2 * BT * D]\
            .rearrange("p (q t f) -> p q t f", q=2, f=D)
        h_turned = work[:, :, :].rearrange("p q n -> p (q n)")[:, free + 2 * BT * D:free + 4 * BT * D]\
            .rearrange("p (q t f) -> p q t f", q=2, f=D)
        assert free + 4 * BT * D <= 4 * TILES * D
        SAMPLES = PER // STRIDE
        sample_i = z_sb[0:SP_, :, :].rearrange("p n f -> p (n f)").bitcast(I32)[:, P:P + SAMPLES]
        sample_f = z_sb[0:SP_, :, :].rearrange("p n f -> p (n f)")[:, 2 * P:2 * P + SAMPLES]
        NW = NT * WINDOWS
        SB = 5
        less = cell_hot[0:SP_, :, :, :].rearrange("p q k c -> p (q k c)")[:, 0:2 * SB * NW]\
            .rearrange("p (q s n) -> p q s n", q=2, s=SB)
        ones_b = low_hot[0:SP_, 0, 0, 0:1]
        window_no = low_hot.bitcast(F16)[0:SP_, 1, :, :].rearrange("p k n -> p (k n)")[:, 0:NW]
        assert SAMPLES % SB == 0 and NW <= WK * P and 2 * SB * NW <= 2 * WK * CELLS and SAMPLES <= P
        assert 3 * P <= NT * HID
        pad = base_i[0:1, :]
        PAD = CHUNKS * CHUNK - E
        HEAD = (CHUNKS - 1) * CHUNK
        s_src, s_f, s_fs, s_less, s_sum = (sem(n) for n in ("src_loaded", "fields_ready", "fields_stored",
                                                            "less_ready", "samples_summed"))
        s_low = sem("low_parts_ready")
        (y_stats, y_moments, y_roots, y_inverse, y_scales, h_ready, h_kept, y_transposed, y_copied, y_products, y_added,
         y_stored) = (sem("y_" + n) for n in ("stats", "moments", "roots", "inverse", "scales", "h_ready", "h_kept",
                                              "transposed", "copied", "products", "added", "stored"))
        y_turn, y_acc = [(0, 1), (6, 7)], [(2, 3), (4, 5)]

        with nc.Block() as block:
            @block.sync
            def _(sp):
                sp.dma_start(dst_i, dst.rearrange("(p k) -> p k", p=SP_)).then_inc(s_dst, 16)
                sp.dma_start(src_i, src.rearrange("(p k) -> p k", p=SP_)).then_inc(s_src, 16)
                for k in range(NB):
                    hi = min((k + 1) * BT, FULL)
                    sp.dma_start(x_sb[:, k * BT:hi, :],
                                 x[k * BT * P:hi * P, :].rearrange("(t p) f -> p t f", p=P)).then_inc(s_x, 16)
                sp.wait_ge(s_vc, 1)
                sp.dma_start(x_sb[0:TAIL, FULL, :], x[FULL * P:N, :]).then_inc(s_x, 16)
                sp.dma_start(dst_any[0:HEAD].rearrange("(a b) -> a b", a=CHUNKS - 1),
                             dst[0:HEAD].rearrange("(a b) -> a b", a=CHUNKS - 1)).then_inc(s_any, 16)
                sp.dma_start(dst_any[HEAD + PAD:], dst[HEAD:]).then_inc(s_any, 16)
                sp.wait_ge(s_f, 3)
                sp.dma_start(fields.rearrange("(p k) c -> p k c", p=SP_), field_f).then_inc(s_fs, 16)
                sp.wait_ge(s_pad, 1)
                at = HEAD
                while at < HEAD + PAD:
                    n = min(NT, HEAD + PAD - at)
                    sp.dma_start(dst_any[at:at + n].unsqueeze(0), pad[:, 0:n]).then_inc(s_any, 16)
                    at += n

                def emit(b, q):
                    sp.wait_ge(y_added, b + 1)
                    sp.sem_inc(stood, 1)
                    sp.dma_start(y_table[bass.ds(b * BT * P, BT * P), :].rearrange("(t p) f -> p t f", p=P),
                                 agg[:, bass.ds(b * BT, BT), 0:D]).then_inc(y_stored, 16)

                over_batches(sp, emit)
                sp.wait_ge(s_any, 16 * (2 + -(-PAD // NT)))
                sp.wait_ge(s_fs, 16)
                sp.wait_ge(y_stored, 16 * NB)

            @block.scalar
            def _(act):
                for to, of in ([
                        (wm_top, W_msg[0:D, :]), (wm_bot, W_msg[D:, :]), (wu_top, W_upd[0:D, :]),
                        (wu_bot, W_upd[D:, :]), (w1_sb, W1), (w2_sb, W2)]):
                    act.dma_start(to[:, :], of).then_inc(s_w, 16)
                for to, of in ((bm_sb, b_msg), (bu_sb, b_upd), (gm_sb, gamma), (be_sb, beta), (b2_sb, b2), (b1_sb, b1)):
                    act.dma_start(to[:, :], of.partition_broadcast(P)).then_inc(s_w, 16)

                def emit(b, q):
                    act.wait_ge(y_moments, b + 1)
                    act.activation(roots[:, q, :], moments[:, q, :, 1], ACT.Sqrt, bias=eps[:, 0:1]).then_inc(y_roots, 1)
                    normal(b - 1, 1 - q)
                    copy_turned(b - 2, q)

                def normal(b, q):
                    if is_first(b, 0):
                        return
                    act.wait_ge(y_scales, b + 1)
                    at_least(act, h_kept, b - 1)
                    for t in range(BT):
                        last = act.activation(h_now_b[:, q, t, :], column_of(x_sb, b * BT + t), ACT.Relu,
                                              bias=shifts[:, q, t:t + 1], scale=scales[:, q, t:t + 1])
                    last.then_inc(h_ready, 1)

                def copy_turned(b, q):
                    if is_first(b, 0):
                        return
                    act.wait_ge(y_transposed, b + 1)
                    at_least(act, y_products, b - 1)
                    lo, hi = y_turn[q]
                    act.copy(h_turned[:, q, 0:GT, :], block_of(lo, GT))
                    act.copy(h_turned[:, q, GT:BT, :], block_of(hi, BT - GT)).then_inc(y_copied, 1)

                over_batches(act, emit)
                normal(NB - 1, (NB - 1) % 2)
                copy_turned(NB - 2, (NB - 2) % 2)
                copy_turned(NB - 1, (NB - 1) % 2)
                act.wait_ge(s_w, 16 * 12)

            @block.gpsimd
            def _(pool):
                pool.memset(ident[:, :], 0.0).then_inc(s_pc, 1)
                pool.iota(iota_i[:, :], pattern=[[1, P]], base=0, channel_multiplier=0)
                pool.iota(base_i[:, :], pattern=[[P, NT]], base=0, channel_multiplier=0)
                pool.iota(cell_i[:, :], pattern=[[1, CELLS]], base=1, channel_multiplier=0)
                pool.iota(window_i[:, :, :], pattern=[[SUB, WINDOWS], [0, WK]], base=0, channel_multiplier=0)\
                    .then_inc(s_pc, 1)
                pool.wait_ge(s_pc, 1)
                pool.affine_select(out=ident[:, :], in_=ident[:, :], compare_op=ALU.not_equal, fill=1.0, base=0,
                                   pattern=[[-1, P]], channel_multiplier=1).then_inc(s_pc, 1)
                pool.wait_ge(s_vc, 3)
                pool.memset(pad, -1).then_inc(s_pad, 1)
                pool.wait_ge(s_dst, 16)
                pool.tensor_copy(field_f[:, :, 0], dst_i).then_inc(s_f, 1)
                pool.wait_ge(s_low, 1)
                pool.tensor_copy(field_f[:, :, 2], low_i).then_inc(s_f, 1)

                def emit(b, q):
                    pool.wait_ge(h_ready, b + 1)
                    pool.sem_inc(stood, 1)
                    pool.tensor_copy(h_sb[:, bass.ds(b * BT, BT), :], h_now_b[:, q, :, :]).then_inc(h_kept, 1)

                over_batches(pool, emit)

            @block.vector
            def _(dve):
                dve.memset(x_sb[:, FULL, :], 0.0).then_inc(s_vc, 1)
                dve.memset(ones[:, :], 1.0).then_inc(s_vc, 1)
                dve.memset(zero[:, :], 0.0)
                dve.memset(ones_b, 1.0)
                dve.memset(eps[:, :], EPS)
                dve.memset(neg_exact[:, :], -EXACT)
                dve.memset(zeros[:, :, :], 0.0)
                dve.memset(msgs[:, :, :, D:D + 1], 1.0)
                dve.wait_ge(s_pc, 3)
                dve.tensor_copy(iota[:, :], iota_i[:, :])
                dve.tensor_copy(iota_b[:, :], iota_i[:, :])
                dve.tensor_copy(cell_key[:, :], cell_i[:, :])
                dve.tensor_copy(window_base[:, :, :], window_i[:, :, :])
                dve.tensor_scalar(window_no, cell_i[0:SP_, 0:NW], 1.0, None, ALU.subtract)
                dve.tensor_copy(node_base[:, :], base_i[:, :]).then_inc(s_vc, 1)
                dve.wait_ge(s_vc, 3)
                dve.wait_ge(s_dst, 16)
                every = dst_i.rearrange("p (k s) -> p k s", s=STRIDE)[:, :, 0]
                dve.tensor_scalar(sample_i, every, 4, None, ALU.logical_shift_right).then_inc(s_vc, 1)
                assert SUB == 1 << 4
                dve.wait_ge(s_vc, 4)
                dve.tensor_copy(sample_f, sample_i).then_inc(s_vc, 1)
                dve.wait_ge(s_vc, 5)
                for n in range(SAMPLES // SB):
                    if n >= 2:
                        dve.wait_ge(s_sum, n - 1)
                    for j in range(SB):
                        sample = sample_f[:, n * SB + j:n * SB + j + 1]
                        last = dve.tensor_scalar(less[:, n % 2, j, :], window_no, sample, None, ALU.is_gt)
                    last.then_inc(s_less, 1)
                dve.wait_ge(s_src, 16)
                dve.tensor_scalar(low_i, src_i, P - 1, None, ALU.bitwise_and).then_inc(s_low, 1)
                dve.tensor_scalar(high_i, src_i, 7, None, ALU.logical_shift_right).then_inc(s_vc, 1)
                dve.wait_ge(s_vc, 6)
                dve.tensor_scalar(field_f[:, :, 1], high_i, float(SUB), 1.0, ALU.mult, ALU.add).then_inc(s_f, 1)
                dve.wait_ge(s_sum, SAMPLES // SB)
                dve.tensor_scalar(starts_f[:, :], bank[4][0:1, 0:NW], float(STRIDE), float(-STRIDE), ALU.mult, ALU.add)\
                   .then_inc(s_vc, 1)
                dve.wait_ge(s_vc, 7)
                dve.tensor_scalar(starts[:, :], starts_f[:, :].rearrange("p (n w) -> p n w", w=WINDOWS)[:, :, 0],
                                  0.0, float(LAST_START), ALU.max, ALU.min)
                dve.tensor_scalar(window_starts[:, :], starts_f[:, :], 0.0, float(E - WEDGES), ALU.max, ALU.min)\
                   .then_inc(s_st, 1)
                dve.wait_ge(s_x, 16 * (NB + 1))

                def emit(b, q):
                    for t in range(BT):
                        last = dve.bn_stats(stats[:, q, t, :], column_of(x_sb, b * BT + t))
                    last.then_inc(y_stats, 1)
                    dve.wait_ge(y_stats, b + 1)
                    dve.sem_inc(stood, 1)
                    for t in range(BT):
                        last = dve.bn_aggr(moments[:, q, t, :], stats[:, q, t, :])
                    last.then_inc(y_moments, 1)
                    scale(b - 1, 1 - q)
                    add_row(b - 3, 1 - q)

                def scale(b, q):
                    if is_first(b, 0):
                        return
                    dve.wait_ge(y_roots, b + 1)
                    dve.reciprocal(scales[:, q, :], roots[:, q, :]).then_inc(y_inverse, 1)
                    dve.wait_ge(y_inverse, b + 1)
                    dve.scalar_tensor_tensor(shifts[:, q, :], moments[:, q, :, 0], -1.0, scales[:, q, :], ALU.mult,
                                             ALU.mult).then_inc(y_scales, 1)

                def add_row(b, q):
                    if is_first(b, 0):
                        return
                    dve.wait_ge(y_products, b + 1)
                    lo, hi = y_acc[q]
                    dve.tensor_tensor(agg[:, bass.ds(b * BT, GT), 0:D], block_of(lo, GT), over(bm_sb[:, :], GT),
                                      ALU.add)
                    dve.tensor_tensor(agg[:, bass.ds(b * BT + GT, BT - GT), 0:D], block_of(hi, BT - GT),
                                      over(bm_sb[:, :], BT - GT), ALU.add).then_inc(y_added, 1)

                dve.wait_ge(s_w, 16 * 12)
                over_batches(dve, emit)
                scale(NB - 1, (NB - 1) % 2)
                add_row(NB - 3, (NB - 3) % 2)
                add_row(NB - 2, (NB - 2) % 2)
                add_row(NB - 1, (NB - 1) % 2)

            @block.tensor
            def _(pe):
                pe.wait_ge(s_vc, 3)
                for n in range(SAMPLES // SB):
                    pe.wait_ge(s_less, n + 1)
                    for j in range(SB):
                        last = pe.matmul(bank[4][0:1, 0:NW], ones_b, less[:, n % 2, j, :],
                                         start=n + j == 0, stop=n * SB + j == SAMPLES - 1)
                    last.then_inc(s_sum, 1)

                def emit(b, q):
                    turn(b - 1, 1 - q)
                    multiply(b - 2, q)

                def turn(b, q):
                    if is_first(b, 0):
                        return
                    pe.wait_ge(h_ready, b + 1)
                    at_least(pe, y_copied, b - 1)
                    for t, place in enumerate(halves(*y_turn[q], BT)):
                        last = pe.transpose(place, h_now_b[:, q, t, :], ident[:, :])
                    last.then_inc(y_transposed, 1)

                def multiply(b, q):
                    if is_first(b, 0):
                        return
                    pe.wait_ge(y_copied, b + 1)
                    at_least(pe, y_added, b - 1)
                    for t, place in enumerate(halves(*y_acc[q], BT)):
                        last = pe.matmul(place, h_turned[:, q, t, :], wm_top[:, :], start=True, stop=True)
                    last.then_inc(y_products, 1)

                pe.wait_ge(s_w, 16 * 12)
                over_batches(pe, emit)
                turn(NB - 1, (NB - 1) % 2)
                multiply(NB - 2, (NB - 2) % 2)
                multiply(NB - 1, (NB - 1) % 2)

        s_v = sem("vector_steps_b")
        s_var = sem("variance_ready")
        s_std = sem("deviation_ready")
        s_tr = sem("transposes_done")
        s_ev = sem("transposes_copied")
        s_mm = sem("products_done")
        s_res = sem("result_ready")
        s_st = sem("result_stored")
        dense_sems = [s_v, s_var, s_std, s_tr, s_ev, s_mm, s_res, s_st]

        class Chain:
            def __init__(self, eng, s):
                self.eng, self.s, self.n = eng, s, 0

            def __call__(self, ins):
                self.n += 1
                ins.then_inc(self.s, 1)
                self.eng.wait_ge(self.s, self.n)

        def normalize(dve, step, of, to, scratch, nth):
            step(dve.tensor_reduce(stat[:, 0, :], of, AX.X, ALU.add))
            step(dve.tensor_scalar(stat[:, 1, :], stat[:, 0, :], -1.0 / D, None, ALU.mult))
            step(dve.tensor_tensor(to, of, wide(stat[:, 1, :]), ALU.add))
            step(dve.tensor_tensor(scratch, to, to, ALU.mult))
            step(dve.tensor_reduce(stat[:, 0, :], scratch, AX.X, ALU.add))
            dve.tensor_scalar(stat[:, 2, :], stat[:, 0, :], 1.0 / D, None, ALU.mult).then_inc(s_var, 1)
            dve.wait_ge(s_std, nth)
            step(dve.reciprocal(stat[:, 1, :], stat[:, 3, :]))
            step(dve.tensor_tensor(to, to, wide(stat[:, 1, :]), ALU.mult))

        def deviation(act, nth):
            act.wait_ge(s_var, nth)
            act.activation(stat[:, 3, :], stat[:, 2, :], ACT.Sqrt, bias=eps[:, 0:1]).then_inc(s_std, 1)

        def transpose_batch(pe, of, a, b):
            for t, place in enumerate(halves(a, b, BT)):
                last = pe.transpose(place, of[:, t, :], ident[:, :])
            return last

        def copy_batch(act, to, a, b):
            act.copy(to[:, 0:GT, :], block_of(a, GT))
            return act.copy(to[:, GT:BT, :], block_of(b, BT - GT))

        def add_banks(dve, step, to, a, b, row):
            dve.tensor_tensor(to[:, 0:GT, :], block_of(a, GT), over(row[:, :], GT), ALU.add)
            step(dve.tensor_tensor(to[:, GT:BT, :], block_of(b, BT - GT), over(row[:, :], BT - GT), ALU.add))

        g_names = ("rows_loaded", "edges_loaded", "rows_gathered",
                   "hot_ready", "edges_transposed", "edges_copied", "products", "messages", "scattered", "chunk_steps",
                   "summed")
        g = {n: sem("g_" + n) for n in g_names}

        def chunk_block(kind, table, start, dst_rows, node):
            width = D if kind == "message" else HID
            to = gathered[:, 0, :, 0:width] if kind == "message" else \
                gathered[:, 0, :, :].rearrange("p t f -> p (t f)")[:, 0:TILES * HID].rearrange("p (t f) -> p t f", f=HID)
            with nc.Block() as block:
                @block.sync
                def _(sp):
                    s = start(sp)
                    sp.dma_start(rows[:, 0, 0, :], src[bass.ds(s, CHUNK)].rearrange("(p j) -> p j", p=P))\
                      .then_inc(g["rows_loaded"], 16)
                    sp.dma_start(rows[:, 0, 1, :], dst_rows(s)).then_inc(g["rows_loaded"], 16)
                    if kind == "message":
                        sp.dma_start(edges[:, 0, :, :].rearrange("p j f -> p (j f)"),
                                     edge_attr[bass.ds(s, CHUNK), :].rearrange("(p j) f -> p (j f)", p=P))\
                          .then_inc(g["edges_loaded"], 16)

                @block.gpsimd
                def _(pool):
                    pool.wait_ge(g["rows_loaded"], 32)
                    for j in range(TILES):
                        pool.indirect_dma_start(to[:, j, :], None, table[:, :],
                                                bass.IndirectOffsetOnAxis(ap=rows[:, 0, 0, j:j + 1], axis=0))\
                            .then_inc(g["rows_gathered"], 16)
                    pool.wait_ge(g["rows_gathered"], 16 * TILES)

                @block.vector
                def _(dve):
                    step = Chain(dve, g["chunk_steps"])
                    dve.wait_ge(g["rows_loaded"], 32)
                    step(dve.tensor_tensor(dst_loc[:, 0, :], rows[:, 0, 1, :],
                                           node_base[:, bass.ds(node, 1)].to_broadcast([P, TILES]), ALU.subtract))
                    for n, (j, k) in enumerate(GROUPS):
                        if n:
                            dve.wait_ge(g["scattered"], n)
                        dve.tensor_tensor(hot[:, 0, 0:k, :], over(iota[:, :], k), wide(dst_loc[:, 0, j:j + k], P),
                                          ALU.is_equal).then_inc(g["hot_ready"], 1)
                        if n == 0:
                            dve.wait_ge(g["rows_gathered"], 16 * TILES)
                        if kind == "message":
                            dve.wait_ge(g["products"], n + 1)
                            pr = msgs[:, 1, 0:k, 0:D]
                            step(dve.tensor_tensor(pr, block_of(1, k), to[:, j:j + k, :], ALU.add))
                            dve.tensor_scalar(msgs[:, 0, 0:k, 0:D], pr, 0.0, None, ALU.max).then_inc(g["messages"], 1)
                    dve.wait_ge(g["scattered"], NG)
                    sums = agg if kind == "message" else conv
                    n = sums.shape[2]
                    dve.tensor_tensor(sums[:, bass.ds(node, 1), :].rearrange("p a f -> p (a f)"),
                                      sums[:, bass.ds(node, 1), :].rearrange("p a f -> p (a f)"),
                                      bank[4][:, 0:n], ALU.add).then_inc(g["summed"], 1)

                @block.scalar
                def _(act):
                    if kind == "message":
                        for n, (j, k) in enumerate(GROUPS):
                            act.wait_ge(g["edges_transposed"], n + 1)
                            act.copy(edges_T[:, 0, 0:k * P], bank[0][:, 0:k * P]).then_inc(g["edges_copied"], 1)

                @block.tensor
                def _(pe):
                    if kind == "message":
                        pe.wait_ge(g["edges_loaded"], 16)
                    else:
                        pe.wait_ge(g["rows_gathered"], 16 * TILES)
                    for n, (j, k) in enumerate(GROUPS):
                        if kind == "message":
                            for t in range(k):
                                last = pe.transpose(bank[0][:, t * P:t * P + P], edges[:, 0, j + t, :], ident[:, :])
                            last.then_inc(g["edges_transposed"], 1)
                            pe.wait_ge(g["edges_copied"], n + 1)
                            for t in range(k):
                                last = pe.matmul(bank[1][:, t * D:t * D + D], edges_T[:, 0, t * P:t * P + P],
                                                 wm_bot[:, :], start=True, stop=True)
                            last.then_inc(g["products"], 1)
                            pe.wait_ge(g["messages"], n + 1)
                        pe.wait_ge(g["hot_ready"], n + 1)
                        for t in range(k):
                            rhs = msgs[:, 0, t, :] if kind == "message" else to[:, j + t, :]
                            last = pe.matmul(bank[4][:, 0:rhs.shape[1]], hot[:, 0, t, :], rhs,
                                             start=j + t == 0, stop=j + t == TILES - 1)
                        last.then_inc(g["scattered"], 1)
            nc.gpsimd.dma_reset(range(g["rows_gathered"].num, g["rows_gathered"].num + 1))
            clear(list(g.values()))

        def pass_over_all(kind, table):
            with nc.Fori(0, NT) as i:
                with nc.Block() as block:
                    @block.vector
                    def _(dve):
                        sums = (agg if kind == "message" else conv)[:, bass.ds(i, 1), :]
                        dve.tensor_copy(sums, zeros[:, :, 0:sums.shape[2]])
                with nc.Fori(0, CHUNKS - 1) as c:
                    chunk_block(kind, table, lambda sp: c * CHUNK,
                                lambda s: dst_any[bass.ds(s, CHUNK)].rearrange("(p j) -> p j", p=P), i)
                chunk_block(kind, table, lambda sp: LAST_START,
                            lambda s: dst_any[HEAD:HEAD + CHUNK].rearrange("(p j) -> p j", p=P), i)

        def in_sem(name):
            return [sem(f"{name}{q}") for q in range(2)]

        rows_in, keys_in, edges_in = in_sem("rows_in"), in_sem("keys_in"), in_sem("edges_in")
        group_in = [[sem(f"group{n}_in{q}") for n in range(NG)] for q in range(2)]
        cells_stored = sem("cells_stored")
        (transposed, copied, products, added, msgs_ready, hot_ready, scattered, agg_copied, cell_hots, half_done,
         half_copied, columns) = (sem("m_" + n) for n in (
             "transposed", "copied", "products", "added", "msgs_ready", "hot_ready", "scattered", "agg_copied",
             "cell_hots", "half_done", "half_copied", "columns"))
        u1_dve, u1_act, u1_pe, u2_dve, u2_act, u2_pe = (sem(n) for n in (
            "update1_vector", "update1_scalar", "update1_tensor", "update2_vector", "update2_scalar", "update2_tensor"))
        tallied = sem("tallied")
        tp, pm, acc, cell_bank, upd = bank[0:2], bank[2:4], bank[4], bank[5:7], bank[7]
        COLUMNS = 8
        COLUMN_GROUPS = (5, 6)
        H = len(HALVES)
        U1_DVE, U1_ACT, U1_PE, U2_DVE, U2_ACT, U2_PE = 5, 5, 2, 14, 5, 2

        def over_chunks(eng, emit):
            emit(0, 0, 0, True)
            emit(1, 1, 0, True)
            with eng.Fori(1, NT // 2) as i:
                emit(i * 2, 0, i, True)
                emit(i * 2 + 1, 1, i, True)
            emit(NT - 1, 0, NT // 2, False)

        def first_part(k, n, steps):
            return n in steps and not is_first(k, 1) and not (isinstance(k, int) and k > NT)

        def second_part(k, n, steps):
            return n in steps and not is_first(k, 2)

        class Part:
            def __init__(self, s, per, tile):
                self.s, self.per, self.tile = s, per, tile

            def wait(self, eng, n):
                eng.wait_ge(self.s, self.tile * self.per + n)

            def done(self, ins):
                ins.then_inc(self.s, 1)

        def parts_of(m):
            return (Part(u1_dve, U1_DVE, m), Part(u1_act, U1_ACT, m), Part(u1_pe, U1_PE, m),
                    Part(u2_dve, U2_DVE, m), Part(u2_act, U2_ACT, m), Part(u2_pe, U2_PE, m))

        def update_dve(dve, k, n, j):
            if first_part(k, n, (1, 7)):
                d1, a1, p1 = parts_of(k - 1)[0:3]
                if (n, j) == (1, 1):
                    dve.wait_ge(scattered, k * NG)
                    d1.done(dve.tensor_scalar(ut[:, 0:1], acc[:, D:D + 1], 1.0, None, ALU.max))
                    dve.tensor_copy(column_of(agg, k - 1), acc[:, 0:D + 1]).then_inc(agg_copied, 1)
                if (n, j) == (1, 3):
                    d1.wait(dve, 1)
                    d1.done(dve.reciprocal(ut[:, 1:2], ut[:, 0:1]))
                if (n, j) == (7, 2):
                    a1.wait(dve, 4)
                    d1.done(dve.tensor_tensor(u_sb[:, :], u_sb[:, :], bu_sb[:, :], ALU.add))
                if (n, j) == (7, 3):
                    d1.wait(dve, 3)
                    dve.sem_inc(stood, 1)
                    d1.done(dve.bn_stats(ust[:, 0:6], u_sb[:, :]))
                if (n, j) == (7, 4):
                    d1.wait(dve, 4)
                    dve.sem_inc(stood, 1)
                    d1.done(dve.bn_aggr(uag[:, 0:2], ust[:, 0:6]))
            if second_part(k, n, (0, 2, 3, 4, 6, 8)):
                a1 = parts_of(k - 2)[1]
                d2, a2, p2 = parts_of(k - 2)[3:6]
                if (n, j) == (0, 2):
                    a1.wait(dve, 5)
                    d2.done(dve.reciprocal(ut[:, 2:3], ut[:, 3:4]))
                if (n, j) == (0, 3):
                    d2.wait(dve, 1)
                    d2.done(dve.scalar_tensor_tensor(ut[:, 4:5], uag[:, 0:1], -1.0, ut[:, 2:3], ALU.mult, ALU.mult))
                if (n, j) == (2, 1):
                    a2.wait(dve, 1)
                    d2.done(dve.tensor_tensor(u_sb[:, :], u_sb[:, :], gm_sb[:, :], ALU.mult))
                if (n, j) == (2, 2):
                    d2.wait(dve, 3)
                    d2.done(dve.tensor_tensor(u_sb[:, :], u_sb[:, :], be_sb[:, :], ALU.add))
                if (n, j) == (2, 3):
                    d2.wait(dve, 4)
                    d2.done(dve.tensor_tensor(u_sb[:, :], u_sb[:, :], column_of(h_sb, k - 2), ALU.add))
                if (n, j) == (2, 4):
                    d2.wait(dve, 5)
                    d2.done(dve.scalar_tensor_tensor(column_of(x_sb, k - 2), u_sb[:, :], 0.0, column_of(x_sb, k - 2),
                                                     ALU.max, ALU.add))
                if (n, j) == (3, 0):
                    d2.wait(dve, 6)
                    dve.sem_inc(stood, 1)
                    d2.done(dve.bn_stats(ust[:, 6:12], column_of(x_sb, k - 2)))
                if (n, j) == (3, 1):
                    d2.wait(dve, 7)
                    dve.sem_inc(stood, 1)
                    d2.done(dve.bn_aggr(uag[:, 2:4], ust[:, 6:12]))
                if (n, j) == (4, 1):
                    a2.wait(dve, 2)
                    d2.done(dve.reciprocal(ut[:, 5:6], ut[:, 6:7]))
                if (n, j) == (4, 2):
                    d2.wait(dve, 9)
                    d2.done(dve.scalar_tensor_tensor(ut[:, 7:8], uag[:, 2:3], -1.0, ut[:, 5:6], ALU.mult, ALU.mult))
                if (n, j) == (4, 3):
                    dve.wait_ge(agg_copied, k - 1)
                    d2.done(dve.tensor_scalar(ut[:, 8:9], column_of(agg, k - 2)[:, D:D + 1], 1.0, None, ALU.add))
                if (n, j) == (6, 1):
                    a2.wait(dve, 4)
                    d2.done(dve.reciprocal(ut[:, 10:11], ut[:, 9:10]))
                if (n, j) == (6, 3):
                    d2.wait(dve, 12)
                    d2.done(dve.tensor_copy(dinv[:, bass.ds(k - 2, 1)], ut[:, 10:11]))
                if (n, j) == (8, 3):
                    p2.wait(dve, 2)
                    d2.done(dve.tensor_scalar(column_of(z_sb, k - 2), upd[:, 0:HID], ut[:, 10:11], None, ALU.mult))

        def update_act(act, k, n):
            if first_part(k, n, (2, 4, 6, 8)):
                d1, a1, p1 = parts_of(k - 1)[0:3]
                if n == 2:
                    d1.wait(act, 2)
                    act.wait_ge(agg_copied, k)
                    a1.done(act.activation(mean_sb[:, :], column_of(agg, k - 1)[:, 0:D], ACT.Copy, scale=ut[:, 1:2]))
                    a1.done(act.copy(h_now[:, :], column_of(h_sb, k - 1)))
                if n == 4:
                    p1.wait(act, 1)
                    a1.done(act.copy(tu_sb[:, :], upd[:, 0:2 * D]))
                if n == 6:
                    p1.wait(act, 2)
                    a1.done(act.copy(u_sb[:, :], upd[:, 2 * D:3 * D]))
                if n == 8:
                    d1.wait(act, 5)
                    a1.done(act.activation(ut[:, 3:4], uag[:, 1:2], ACT.Sqrt, bias=eps[:, 0:1]))
            if second_part(k, n, (1, 3, 4, 6)):
                d2, a2, p2 = parts_of(k - 2)[3:6]
                if n == 1:
                    d2.wait(act, 2)
                    a2.done(act.activation(u_sb[:, :], u_sb[:, :], ACT.Identity, bias=ut[:, 4:5], scale=ut[:, 2:3]))
                if n == 3:
                    d2.wait(act, 8)
                    a2.done(act.activation(ut[:, 6:7], uag[:, 3:4], ACT.Sqrt, bias=eps[:, 0:1]))
                if n == 4:
                    d2.wait(act, 11)
                    a2.done(act.activation(h2_sb[:, :], column_of(x_sb, k - 2), ACT.Relu, bias=ut[:, 7:8],
                                           scale=ut[:, 5:6]))
                    a2.done(act.activation(ut[:, 9:10], ut[:, 8:9], ACT.Sqrt, bias=zero[:, 0:1]))
                if n == 6:
                    p2.wait(act, 1)
                    a2.done(act.copy(h2t_sb[:, :], upd[:, 3 * D:4 * D]))

        def update_pe(pe, k, n):
            if first_part(k, n, (3,)):
                d1, a1, p1 = parts_of(k - 1)[0:3]
                a1.wait(pe, 2)
                if not is_first(k, 2):
                    parts_of(k - 2)[3].wait(pe, 2)
                pe.transpose(upd[:, 0:D], mean_sb[:, :], ident[:, :])
                p1.done(pe.transpose(upd[:, D:2 * D], h_now[:, :], ident[:, :]))
            if second_part(k, n, (5,)):
                d2, a2, p2 = parts_of(k - 2)[3:6]
                a2.wait(pe, 3)
                if first_part(k, n, (5,)):
                    parts_of(k - 1)[1].wait(pe, 3)
                p2.done(pe.transpose(upd[:, 3 * D:4 * D], h2_sb[:, :], ident[:, :]))
            if first_part(k, n, (5,)):
                d1, a1, p1 = parts_of(k - 1)[0:3]
                a1.wait(pe, 3)
                pe.matmul(upd[:, 2 * D:3 * D], tu_sb[:, D:2 * D], wu_top[:, :], start=True, stop=False)
                p1.done(pe.matmul(upd[:, 2 * D:3 * D], tu_sb[:, 0:D], wu_bot[:, :], start=False, stop=True))
            if second_part(k, n, (7,)):
                d2, a2, p2 = parts_of(k - 2)[3:6]
                a2.wait(pe, 5)
                p2.done(pe.matmul(upd[:, 0:HID], h2t_sb[:, :], w1_sb[:, :], start=True, stop=True))

        SLOT = QT * COUNTS
        assert QUADS % RING == 0 and ROUNDS >= 2 and QUADS * QT == FULL and NT - FULL == 1
        in_chunks = work[:, :, :].rearrange("p q n -> p (q n)").bitcast(FP8)
        in_agg = agg[:, :, :].rearrange("p n f -> p (n f)").bitcast(FP8)
        PAIR = 2 * TILES * D * 4
        slots = [in_chunks[:, 0:SLOT], in_chunks[:, PAIR:PAIR + SLOT], in_agg[:, 0:SLOT]]
        slot_in = [sem(f"slot_in{u}") for u in range(RING)]
        in_h = h_sb[:, :, :].rearrange("p n f -> p (n f)").bitcast(FP8)
        BEHIND = 2 * NT * PARTS * HID * 2
        assert SLOT + COUNTS <= PAIR and BEHIND + 2 * COUNTS <= NT * D * 4 and QT == 4
        kept = [in_chunks[:, SLOT:SLOT + COUNTS], in_chunks[:, PAIR + SLOT:PAIR + SLOT + COUNTS],
                in_h[:, BEHIND:BEHIND + COUNTS], in_h[:, BEHIND + COUNTS:BEHIND + 2 * COUNTS]]
        kept_in = sem("kept_in")

        def load_kept(sp, t):
            return sp.dma_start(kept[t].bitcast(U8), adjacency[FULL - QT + t, :, :])


        def load_slot(sp, u, first):
            return sp.dma_start(slots[u].bitcast(U8).rearrange("p (t n) -> p t n", t=QT),
                                adjacency[bass.ds(first, QT), :, :].rearrange("t p n -> p t n"))

        with nc.Block() as block:
            @block.sync
            def _(sp):
                def load(k, q):
                    s = sp.value_load(starts[0:1, bass.ds(k, 1)], min_val=0, max_val=LAST_START)
                    sp.dma_start(rows[:, q, 0, :], src[bass.ds(s, CHUNK)].rearrange("(p j) -> p j", p=P))\
                      .then_inc(rows_in[q], 16)
                    sp.dma_start(rows[:, q, 1, :], dst[bass.ds(s, CHUNK)].rearrange("(p j) -> p j", p=P))\
                      .then_inc(rows_in[q], 16)
                    sp.dma_start(edges[:, q, :, :].rearrange("p j f -> p (j f)"),
                                 edge_attr[bass.ds(s, CHUNK), :].rearrange("(p j) f -> p (j f)", p=P))\
                      .then_inc(edges_in[q], 16)
                    for w in range(WINDOWS):
                        s = sp.value_load(window_starts[0:1, bass.ds(k * WINDOWS + w, 1)], min_val=0,
                                          max_val=E - WEDGES)
                        sp.dma_start(keys[:, q, w, :, :].rearrange("p j c -> p (j c)"),
                                     fields[bass.ds(s, WEDGES), :].rearrange("(p j) c -> p (j c)", p=P))\
                          .then_inc(keys_in[q], 16)

                def emit(k, q, i, more):
                    if more:
                        at_least(sp, added, k * NG)
                        at_least(sp, transposed, k * NG)
                        sp.sem_inc(stood, 1)
                        at_least(sp, cell_hots, k * WINDOWS)
                        sp.sem_inc(stood, 1)
                        load(k + 1, 1 - q)
                    else:
                        sp.wait_ge(added, k * NG)
                        sp.wait_ge(transposed, k * NG)
                        sp.wait_ge(cells_stored, 16 * k)
                        load_slot(sp, 1, QT).then_inc(slot_in[1], 16)
                    at_least(sp, half_copied, k * WINDOWS * H + WINDOWS * H)
                    sp.sem_inc(stood, 1)
                    sp.dma_start(adjacency[bass.ds(k, 1), :, :].rearrange("a p n -> (a p) n"),
                                 cells[:, :, :, :].rearrange("p a w d -> p (a w d)").bitcast(U8))\
                      .then_inc(cells_stored, 16)

                load(0, 0)
                over_chunks(sp, emit)
                sp.wait_ge(transposed, NT * NG)
                sp.wait_ge(added, NT * NG)
                load_slot(sp, 0, 0).then_inc(slot_in[0], 16)
                sp.wait_ge(cells_stored, 16 * NT)

            @block.gpsimd
            def _(pool):
                def emit(k, q, i, more):
                    at_least(pool, rows_in[q], i * 32 + 32)
                    at_least(pool, added, k * NG - NG)
                    pool.sem_inc(stood, 1)
                    for n, (j, c) in enumerate(GROUPS):
                        for t in range(j, j + c):
                            pool.indirect_dma_start(gathered[:, q, t, :], None, y_table[:, :],
                                                    bass.IndirectOffsetOnAxis(ap=rows[:, q, 0, t:t + 1], axis=0))\
                                .then_inc(group_in[q][n], 16)

                over_chunks(pool, emit)

            @block.vector
            def _(dve):
                def find_columns(k, q, i, m):
                    base = node_base[:, bass.ds(k, 1)]
                    d, inside = key_tmp[:, 0, :, :], key_tmp[:, 1, :, :]
                    if m == 0:
                        at_least(dve, rows_in[q], i * 32 + 32)
                        ins = dve.tensor_scalar(dst_loc[:, q, :], rows[:, q, 1, :], base, None, ALU.subtract)
                    if m == 1:
                        at_least(dve, keys_in[q], i * 16 * WINDOWS + 16 * WINDOWS)
                        ins = dve.tensor_scalar(d, keys[:, q, :, :, 0], base, None, ALU.subtract)
                    if m >= 2:
                        dve.wait_ge(columns, k * COLUMNS + m)
                    if m == 2:
                        ins = dve.tensor_tensor(d, d, window_base[:, :, :], ALU.subtract)
                    if m == 3:
                        ins = dve.tensor_scalar(inside, d, 0.0, None, ALU.is_ge)
                    if m == 4:
                        ins = dve.scalar_tensor_tensor(inside, d, float(SUB), inside, ALU.is_lt, ALU.mult)
                    if m == 5:
                        ins = dve.tensor_tensor(d, d, keys[:, q, :, :, 1], ALU.add)
                    if m == 6:
                        ins = dve.tensor_tensor(cell_of[:, q, :, :], d, inside, ALU.mult)
                    if m == 7:
                        ins = dve.tensor_copy(src_low[:, q, :, :], keys[:, q, :, :, 2])
                    ins.then_inc(columns, 1)

                def emit(k, q, i, more):
                    dve.wait_ge(columns, k * COLUMNS + COLUMNS)
                    for n, (j, c) in enumerate(GROUPS):
                        b = (q * NG + n) % 2
                        at_least(dve, scattered, k * NG + (n - 1))
                        dve.tensor_tensor(hot[:, b, 0:c, :], over(iota[:, :], c), wide(dst_loc[:, q, j:j + c], P),
                                          ALU.is_equal).then_inc(hot_ready, 1)
                        if n < WINDOWS:
                            at_least(dve, half_done, k * WINDOWS * H + (n - 1) * H)
                            for t in range(WK):
                                dve.tensor_scalar(cell_hot[:, n % 2, t, :], cell_key[:, :], cell_of[:, q, n, t:t + 1],
                                                  None, ALU.is_equal)
                                between(k, q, i, more, n, t)
                            dve.tensor_tensor(low_hot[:, n % 2, :, :], over(iota_b[:, :], WK),
                                              wide(src_low[:, q, n, :], P), ALU.is_equal).then_inc(cell_hots, 1)
                        else:
                            for t in range(WK):
                                between(k, q, i, more, n, t)
                        if n == 3 and not is_first(k, 1):
                            add_tally(k, 1 - q)
                        dve.wait_ge(products, k * NG + (n + 1))
                        dve.wait_ge(group_in[q][n], i * 16 * c + 16 * c)
                        dve.tensor_tensor(msgs[:, b, 0:c, 0:D],
                                          pm[b][:, 0:c * D].rearrange("p (t f) -> p t f", f=D),
                                          gathered[:, q, j:j + c, :], ALU.add).then_inc(added, 1)

                def between(k, q, i, more, n, j):
                    update_dve(dve, k, n, j)
                    if more and n in COLUMN_GROUPS and j < COLUMNS // len(COLUMN_GROUPS):
                        find_columns(k + 1, 1 - q, i + q, COLUMN_GROUPS.index(n) * (COLUMNS // len(COLUMN_GROUPS)) + j)

                def add_tally(k, q):
                    dve.wait_ge(half_copied, k * WINDOWS * H)
                    dve.wait_ge(tallied, k)
                    dve.tensor_tensor(tallies[:, :, :], tallies[:, :, :], tally[:, q, :, :], ALU.add)\
                       .then_inc(tallied, 1)

                dve.memset(tallies[:, :, :], 0.0).then_inc(tallied, 1)
                for m in range(COLUMNS):
                    find_columns(0, 0, 0, m)
                over_chunks(dve, emit)
                add_tally(NT, (NT - 1) % 2)
                for k in (NT, NT + 1):
                    for n in range(NG):
                        for j in range(WK):
                            update_dve(dve, k, n, j)

            @block.scalar
            def _(act):
                def copy_group(k, q, n):
                    b, c = (q * NG + n) % 2, GROUPS[n][1]
                    act.wait_ge(transposed, k * NG + (n + 1))
                    at_least(act, products, k * NG + (n - 1))
                    act.copy(edges_T[:, b, 0:c * P], tp[b][:, 0:c * P]).then_inc(copied, 1)

                def emit(k, q, i, more):
                    for n, (j, c) in enumerate(GROUPS):
                        b = (q * NG + n) % 2
                        if 1 <= n <= WINDOWS:
                            half_window(k, q, n - 1, 0)
                        if n + 1 < NG:
                            copy_group(k, q, n + 1)
                        elif more:
                            copy_group(k + 1, 1 - q, 0)
                        if 1 <= n <= WINDOWS:
                            half_window(k, q, n - 1, 1)
                        act.wait_ge(added, k * NG + (n + 1))
                        act.activation(msgs[:, b, 0:c, 0:D], msgs[:, b, 0:c, 0:D], ACT.Relu).then_inc(msgs_ready, 1)
                        update_act(act, k, n)

                def half_window(k, q, w, h):
                    lo, hi = HALVES[h]
                    col = w * H + h
                    act.wait_ge(half_done, k * WINDOWS * H + (col + 1))
                    if col == 0:
                        at_least(act, cells_stored, k * 16)
                    act.sem_inc(stood, 1)
                    act.activation(cells[:, lo // SUB:hi // SUB, w, :],
                                   cell_bank[h][:, 0:hi - lo].rearrange("p (a d) -> p a d", d=SUB), ACT.Copy,
                                   accum_out=tally[:, q, 0, col:col + 1], saturate=False)
                    at_least(act, half_copied, k * WINDOWS * H + (col - 1))
                    act.activation(over_junk[:, h, 0:hi - lo], cell_bank[h][:, 0:hi - lo], ACT.Relu,
                                   bias=neg_exact[:, 0:1], accum_out=tally[:, q, 1, col:col + 1])\
                       .then_inc(half_copied, 1)

                copy_group(0, 0, 0)
                over_chunks(act, emit)
                for k in (NT, NT + 1):
                    for n in range(NG):
                        update_act(act, k, n)

            @block.tensor
            def _(pe):
                def transpose_group(k, q, i, n):
                    b, (j, c) = (q * NG + n) % 2, GROUPS[n]
                    if n == 0:
                        pe.wait_ge(edges_in[q], i * 16 + 16)
                    at_least(pe, copied, k * NG + (n - 1))
                    for t in range(c):
                        last = pe.transpose(tp[b][:, t * P:t * P + P], edges[:, q, j + t, :], ident[:, :])
                    last.then_inc(transposed, 1)

                def scatter(k, b, n):
                    j, c = GROUPS[n - 1]
                    pe.wait_ge(msgs_ready, k * NG + n)
                    pe.wait_ge(hot_ready, k * NG + n)
                    if n == 1:
                        at_least(pe, agg_copied, k)
                    for t in range(c):
                        last = pe.matmul(acc[:, 0:D + 1], hot[:, 1 - b, t, :], msgs[:, 1 - b, t, :],
                                         start=j + t == 0, stop=j + t == TILES - 1)
                    last.then_inc(scattered, 1)

                def emit(k, q, i, more):
                    for n, (j, c) in enumerate(GROUPS):
                        b = (q * NG + n) % 2
                        if 1 <= n <= WINDOWS:
                            half(k, n - 1, 0)
                        pe.wait_ge(copied, k * NG + (n + 1))
                        at_least(pe, added, k * NG + (n - 1))
                        for t in range(c):
                            last = pe.matmul(pm[b][:, t * D:t * D + D], edges_T[:, b, t * P:t * P + P],
                                             wm_bot[:, :], start=True, stop=True)
                        last.then_inc(products, 1)
                        if n + 1 < NG:
                            transpose_group(k, q, i, n + 1)
                        elif more:
                            transpose_group(k + 1, 1 - q, i + q, 0)
                        if 1 <= n <= WINDOWS:
                            half(k, n - 1, 1)
                        if n > 0 or not is_first(k, 1):
                            scatter(k, b, n)
                        update_pe(pe, k, n)

                def half(k, w, h):
                    lo, hi = HALVES[h]
                    if h == 0:
                        pe.wait_ge(cell_hots, k * WINDOWS + (w + 1))
                    at_least(pe, half_copied, k * WINDOWS * H + (w * H + h - 1))
                    for t in range(WK):
                        last = pe.matmul(cell_bank[h][:, 0:hi - lo], low_hot[:, w % 2, t, :],
                                         cell_hot[:, w % 2, t, lo:hi], start=t == 0, stop=t == WK - 1)
                    last.then_inc(half_done, 1)

                transpose_group(0, 0, 0, 0)
                over_chunks(pe, emit)
                scatter(NT, NT * NG % 2, 0)
                for k in (NT, NT + 1):
                    for n in range(NG):
                        update_pe(pe, k, n)

        s_c, s_m, s_ms = sem("miss_columns"), sem("miss_summed"), sem("miss_set")
        with nc.Block() as block:
            @block.vector
            def _(dve):
                dve.tensor_reduce(miss_col[:, 0:1], agg[:, :, D:D + 1].rearrange("p n a -> p (n a)"), AX.X, ALU.add)
                dve.tensor_reduce(miss_col[:, 1:2], tallies[:, 0, :], AX.X, ALU.add)
                dve.tensor_reduce(miss_col[:, 2:3], tallies[:, 1, :], AX.X, ALU.add).then_inc(s_c, 1)
                dve.wait_ge(s_m, 1)
                dve.tensor_scalar(miss[:, :], bank[0][0:1, 0:2], -1.0, float(E), ALU.mult, ALU.add).then_inc(s_ms, 1)
                dve.wait_ge(s_ms, 1)
                dve.tensor_tensor(miss[:, 1:2], miss[:, 1:2], bank[0][0:1, 2:3], ALU.add).then_inc(s_ms, 1)
                dve.wait_ge(s_ms, 2)

            @block.tensor
            def _(pe):
                pe.wait_ge(s_c, 1)
                pe.matmul(bank[0][0:1, 0:3], ones[:, :], miss_col[:, :], start=True, stop=True).then_inc(s_m, 1)
        missed = nc.values_load(miss[0:1, 0:1], min_val=0, max_val=E)
        inexact = nc.values_load(miss[0:1, 1:2], min_val=0, max_val=2 * E)

        def reload(quad):
            with nc.Fori(0, 1) as once:
                with nc.Block() as block:
                    @block.sync
                    def _(sp):
                        for u in range(2):
                            load_slot(sp, u, (quad + u) * QT).then_inc(s_st, 16)
                            load_kept(sp, u).then_inc(s_st, 16)
                        sp.wait_ge(s_st, 64)
                clear([s_st])

        with nc.If(missed != 0):
            with nc.Fori(0, 1) as once:
                with nc.Block() as block:
                    @block.sync
                    def _(sp):
                        sp.wait_ge(slot_in[0], 16)
                        sp.wait_ge(slot_in[1], 16)
            pass_over_all("message", y_table)
            with nc.Fori(0, 1) as once:
                with nc.Block() as block:
                    @block.sync
                    def _(sp):
                        sp.dma_start(x_sb[:, 0:FULL, :], x[0:FULL * P, :].rearrange("(t p) f -> p t f", p=P))\
                          .then_inc(s_st, 16)
                        sp.dma_start(x_sb[0:TAIL, FULL, :], x[FULL * P:N, :]).then_inc(s_st, 16)
                        sp.wait_ge(s_st, 32)
                clear([s_st])
            with nc.Fori(0, NB) as i:
                tiles = bass.ds(i * BT, BT)
                counts = agg[:, tiles, D:D + 1].rearrange("p n a -> p (n a)")
                with nc.Block() as block:
                    @block.vector
                    def _(dve):
                        step = Chain(dve, s_v)
                        step(dve.tensor_scalar(stat[:, 0, :], counts, 1.0, None, ALU.max))
                        step(dve.reciprocal(stat[:, 1, :], stat[:, 0, :]))
                        step(dve.tensor_tensor(bt0[:, :, :], agg[:, tiles, 0:D], wide(stat[:, 1, :]), ALU.mult))
                        dve.tensor_copy(bt1[:, :, :], h_sb[:, tiles, :]).then_inc(s_res, 1)
                        dve.wait_ge(s_mm, 1)
                        add_banks(dve, step, bt0, 4, 5, bu_sb)
                        normalize(dve, step, bt0[:, :, :], bt1[:, :, :], bt2[:, :, :], 1)
                        step(dve.tensor_tensor(bt1[:, :, :], bt1[:, :, :], over(gm_sb[:, :], BT), ALU.mult))
                        step(dve.tensor_tensor(bt1[:, :, :], bt1[:, :, :], over(be_sb[:, :], BT), ALU.add))
                        step(dve.tensor_tensor(bt1[:, :, :], bt1[:, :, :], h_sb[:, tiles, :], ALU.add))
                        step(dve.tensor_scalar(bt1[:, :, :], bt1[:, :, :], 0.0, None, ALU.max))
                        step(dve.tensor_tensor(x_sb[:, tiles, :], x_sb[:, tiles, :], bt1[:, :, :], ALU.add))
                        normalize(dve, step, x_sb[:, tiles, :], bt0[:, :, :], bt2[:, :, :], 2)
                        step(dve.tensor_scalar(stat[:, 2, :], counts, 1.0, None, ALU.add))
                        dve.tensor_scalar(bt0[:, :, :], bt0[:, :, :], 0.0, None, ALU.max).then_inc(s_res, 1)
                        dve.wait_ge(s_std, 3)
                        step(dve.reciprocal(dinv[:, tiles], stat[:, 3, :]))
                        dve.wait_ge(s_mm, 2)
                        step(dve.tensor_tensor(z_sb[:, tiles, :], block_of(6, BT, HID), wide(dinv[:, tiles], HID), ALU.mult))

                    @block.scalar
                    def _(act):
                        act.wait_ge(s_tr, 1)
                        copy_batch(act, bt2, 0, 1)
                        copy_batch(act, bt3, 2, 3).then_inc(s_ev, 1)
                        deviation(act, 1)
                        deviation(act, 2)
                        act.wait_ge(s_res, 2)
                        act.activation(stat[:, 3, :], stat[:, 2, :], ACT.Sqrt, bias=zero[:, 0:1]).then_inc(s_std, 1)
                        act.wait_ge(s_tr, 2)
                        copy_batch(act, bt1, 0, 1).then_inc(s_ev, 1)

                    @block.tensor
                    def _(pe):
                        pe.wait_ge(s_res, 1)
                        transpose_batch(pe, bt0, 0, 1)
                        transpose_batch(pe, bt1, 2, 3).then_inc(s_tr, 1)
                        pe.wait_ge(s_ev, 1)
                        for t, place in enumerate(halves(4, 5, BT)):
                            pe.matmul(place, bt3[:, t, :], wu_top[:, :], start=True, stop=False)
                            last = pe.matmul(place, bt2[:, t, :], wu_bot[:, :], start=False, stop=True)
                        last.then_inc(s_mm, 1)
                        pe.wait_ge(s_res, 2)
                        transpose_batch(pe, bt0, 0, 1).then_inc(s_tr, 1)
                        pe.wait_ge(s_ev, 2)
                        for t in range(BT):
                            last = pe.matmul(bank[6][:, t * HID:(t + 1) * HID], bt1[:, t, :], w1_sb[:, :],
                                             start=True, stop=True)
                        last.then_inc(s_mm, 1)
                clear(dense_sems)

            reload(0)

        (split_done, sums_done, sums_read, rows_ready, rows_turned, rows_copied, row_products, out_ready, row_steps,
         out_steps) = (sem("c_" + n) for n in (
             "split_done", "sums_done", "sums_read", "rows_ready", "rows_turned", "rows_copied", "row_products",
             "out_ready", "row_steps", "out_steps"))
        out_stored = [sem(f"out_stored{u}") for u in range(RING)]
        conv_sems = [*slot_in, kept_in, split_done, sums_done, sums_read, row_steps]
        row_sb = u_sb[:, 0:QT * HID].rearrange("p (t f) -> p t f", f=HID)
        row_T = edges_T[0:HID, 0, 0:QT * P]
        results = cell_hot[:, :, :, :].rearrange("p q k c -> p (q k c)").bitcast(F32)[:, 0:RING * QT * D]\
            .rearrange("p (u t f) -> p u t f", u=RING, f=D)

        def split(step, z, r, to):
            step(nc.vector.tensor_copy(to[:, :, 0, :], z))
            step(nc.vector.tensor_tensor(r, z, to[:, :, 0, :], ALU.subtract))
            step(nc.vector.tensor_copy(to[:, :, 1, :], r))
            step(nc.vector.tensor_tensor(r, r, to[:, :, 1, :], ALU.subtract))
            return nc.vector.tensor_copy(to[:, :, 2, :], r)

        def convolve_dense(turn):
            ROW_STEPS = (10, 2)[turn]

            def place(r, u):
                if first_step(r):
                    return 0, FULL, 1
                quad = r * RING + u if turn == 0 else r * -RING + (QUADS - 1 - u)
                return r * RING + (u + 1), quad * QT, QT

            def slot_of(u):
                return u if turn == 0 else RING - 1 - u

            def over_steps(eng, emit):
                emit(-1, RING - 1)
                for u in range(RING):
                    emit(0, u)
                if ROUNDS > 2:
                    with eng.Fori(1, ROUNDS - 1) as r:
                        for u in range(RING):
                            emit(r, u)
                for u in range(RING):
                    emit(ROUNDS - 1, u)

            def before(r, u):
                return (r, u - 1) if u > 0 else (r - 1, RING - 1)

            def first_step(r):
                return isinstance(r, int) and r < 0

            def is_kept(r, u):
                return isinstance(r, int) and (r, u) == ((ROUNDS - 1, RING - 1), (0, 0))[turn]

            with nc.Block() as block:
                @block.sync
                def _(sp):
                    def load_next(r, u):
                        sp.wait_ge(sums_done, place(r, u)[0] + 1)
                        sp.sem_inc(stood, 1)
                        load_slot(sp, slot_of(u), place(r + 1, u)[1]).then_inc(slot_in[slot_of(u)], 16)

                    if turn == 0:
                        load_slot(sp, 2, 2 * QT).then_inc(slot_in[2], 16)
                        if ROUNDS > 2:
                            with sp.Fori(0, ROUNDS - 2) as r:
                                for u in range(RING):
                                    load_next(r, u)
                        for u in range(RING - 1):
                            load_next(ROUNDS - 2, u)
                        for t in range(QT):
                            load_kept(sp, t).then_inc(kept_in, 16)
                    else:
                        sp.sem_inc(slot_in[slot_of(0)], 16)
                        for u in range(1, RING):
                            load_next(0, u)
                        if ROUNDS > 2:
                            with sp.Fori(1, ROUNDS - 1) as r:
                                for u in range(RING):
                                    load_next(r, u)

                @block.tensor
                def _(pe):
                    def emit(r, u):
                        s, first, tiles = place(r, u)
                        if is_kept(r, u):
                            at_least(pe, sums_read, s - (RING - 1))
                            if turn == 0:
                                pe.wait_ge(kept_in, 16 * QT)
                            counts = [kept[t].rearrange("p (a n) -> p a n", a=NT) for t in range(QT)]
                        elif tiles == QT:
                            at_least(pe, slot_in[slot_of(u)], (r + 1) * 16 if turn == 0 else r * 16)
                            at_least(pe, sums_read, s - (RING - 1))
                            pe.sem_inc(stood, 1)
                            in_slot = slots[slot_of(u)].rearrange("p (t a n) -> p t a n", t=QT, a=NT)
                            counts = [in_slot[:, t, :, :] for t in range(QT)]
                        else:
                            counts = [cells[:, :, :, :].rearrange("p a w d -> p a (w d)")]
                        for t in range(tiles):
                            if t == tiles // 2 and turn == 1 and not first_step(r):
                                turn_rows(*before(r, u))
                            for a in range(NT):
                                last = pe.matmul(bank[u][:, t * PARTS * HID:(t + 1) * PARTS * HID], counts[t][:, a, :],
                                                 parts[turn][:, a, :, :].rearrange("p c f -> p (c f)"),
                                                 start=a == 0, stop=a == NT - 1)
                        last.then_inc(sums_done, 1)
                        if turn == 1 and not first_step(r):
                            multiply(*before(r, u))

                    def turn_rows(r, u):
                        s, first, tiles = place(r, u)
                        pe.wait_ge(rows_ready, s + 1)
                        at_least(pe, rows_copied, s)
                        for t in range(tiles):
                            last = pe.transpose(bank[4][0:HID, t * P:(t + 1) * P], row_sb[:, t, :], ident[:, :])
                        last.then_inc(rows_turned, 1)

                    def multiply(r, u):
                        s, first, tiles = place(r, u)
                        pe.wait_ge(rows_copied, s + 1)
                        at_least(pe, out_ready, s - (RING - 1))
                        for t in range(tiles):
                            last = pe.matmul(bank[5 + u][:, t * D:(t + 1) * D], row_T[:, t * P:(t + 1) * P],
                                             w2_sb[:, :], start=True, stop=True)
                        last.then_inc(row_products, 1)

                    if turn == 0:
                        pe.wait_ge(split_done, 1)
                    over_steps(pe, emit)
                    if turn == 1:
                        turn_rows(ROUNDS - 1, RING - 1)
                        multiply(ROUNDS - 1, RING - 1)

                if turn == 1:
                    @block.scalar
                    def _(act):
                        def emit(r, u):
                            s, first, tiles = place(r, u)
                            act.wait_ge(rows_turned, s + 1)
                            at_least(act, row_products, s)
                            act.copy(row_T[:, 0:tiles * P], bank[4][0:HID, 0:tiles * P]).then_inc(rows_copied, 1)
                        over_steps(act, emit)

                @block.vector
                def _(dve):
                    if turn == 0:
                        split(Chain(dve, s_v), z_sb[:, :, :], conv[:, :, :], parts[0]).then_inc(split_done, 1)

                    def emit(r, u):
                        s, first, tiles = place(r, u)
                        done = [0]

                        def step(ins):
                            done[0] += 1
                            ins.then_inc(row_steps, 1)
                            dve.wait_ge(row_steps, s * ROW_STEPS + done[0])

                        nodes = bass.ds(first, tiles)
                        row, by_part = row_sb[:, 0:tiles, :], bank[u][:, 0:tiles * PARTS * HID]
                        dve.wait_ge(sums_done, s + 1)
                        if turn == 1:
                            at_least(dve, rows_turned, s)
                        dve.tensor_reduce(row, by_part.rearrange("p (t c f) -> p t f c", c=PARTS, f=HID), AX.X, ALU.add)\
                           .then_inc(sums_read, 1)
                        dve.wait_ge(sums_read, s + 1)
                        step(dve.tensor_tensor(row, row, (z_sb, conv)[turn][:, nodes, :], ALU.add))
                        step(dve.tensor_tensor(row, row, wide(dinv[:, nodes], HID), ALU.mult))
                        if turn == 0:
                            z = conv[:, nodes, :]
                            step(dve.tensor_tensor(row, row, over(b1_sb[:, :], tiles), ALU.add))
                            step(dve.tensor_scalar(row, row, 0.0, None, ALU.max))
                            step(dve.tensor_tensor(z, row, wide(dinv[:, nodes], HID), ALU.mult))
                            step(split(step, z, row, parts[1][:, nodes, :, :]))
                        else:
                            dve.sem_inc(rows_ready, 1)
                            if not first_step(r):
                                add_rows(*before(r, u))
                        assert done[0] == ROW_STEPS

                    def add_rows(r, u):
                        s, first, tiles = place(r, u)
                        to = results[:, u, 0:tiles, :]
                        dve.wait_ge(row_products, s + 1)
                        at_least(dve, out_stored[u], r * 16 + (16 if u == RING - 1 else 0))
                        dve.tensor_tensor(to, block_of(5 + u, tiles), over(b2_sb[:, :], tiles), ALU.add)\
                           .then_inc(out_steps, 1)
                        dve.wait_ge(out_steps, s + 1)
                        dve.tensor_tensor(to, to, x_sb[:, bass.ds(first, tiles), :], ALU.add).then_inc(out_ready, 1)

                    over_steps(dve, emit)
                    if turn == 1:
                        add_rows(ROUNDS - 1, RING - 1)

                if turn == 1:
                    @block.gpsimd
                    def _(pool):
                        def emit(r, u):
                            s, first, tiles = place(r, u)
                            pool.wait_ge(out_ready, s + 1)
                            pool.sem_inc(stood, 1)
                            if tiles == QT:
                                pool.dma_start(out[bass.ds(first * P, QT * P), :].rearrange("(t p) f -> p t f", p=P),
                                               results[:, u, :, :]).then_inc(out_stored[u], 16)
                            else:
                                pool.dma_start(out[FULL * P:N, :], results[0:TAIL, u, 0, :]).then_inc(out_stored[u], 16)
                        over_steps(pool, emit)
                        pool.wait_ge(out_stored[0], 16 * ROUNDS)
                        pool.wait_ge(out_stored[1], 16 * ROUNDS)
                        pool.wait_ge(out_stored[2], 16 * (ROUNDS + 1))
            if turn == 0:
                clear([*conv_sems, s_v])

        def convolve_any(of):
            with nc.Fori(0, 1) as once:
                with nc.Block() as block:
                    @block.vector
                    def _(dve):
                        if of is not z_sb:
                            dve.tensor_copy(z_sb[:, :, :], of[:, :, :]).then_inc(s_res, 1)
                        else:
                            dve.sem_inc(s_res, 1)

                    @block.sync
                    def _(sp):
                        sp.wait_ge(s_res, 1)
                        sp.dma_start(z_table[:, :].rearrange("(t p) f -> p t f", p=P), z_sb[:, :, :]).then_inc(s_st, 16)
                        sp.wait_ge(s_st, 16)
                clear([s_st, s_res])
            pass_over_all("row", z_table)

        convolve_dense(0)
        with nc.If(inexact != 0):
            convolve_any(z_sb)
            with nc.Fori(0, 1) as once:
                with nc.Block() as block:
                    @block.vector
                    def _(dve):
                        step = Chain(dve, s_v)
                        step(dve.tensor_tensor(conv[:, :, :], conv[:, :, :], z_sb[:, :, :], ALU.add))
                        step(dve.tensor_tensor(conv[:, :, :], conv[:, :, :], wide(dinv[:, :], HID), ALU.mult))
                        step(dve.tensor_tensor(conv[:, :, :], conv[:, :, :], over(b1_sb[:, :], NT), ALU.add))
                        step(dve.tensor_scalar(conv[:, :, :], conv[:, :, :], 0.0, None, ALU.max))
                        step(dve.tensor_tensor(conv[:, :, :], conv[:, :, :], wide(dinv[:, :], HID), ALU.mult))
                        step(split(step, conv[:, :, :], z_sb[:, :, :], parts[1]))
                clear([s_v])
            reload(QUADS - RING)

        convolve_dense(1)
        with nc.If(inexact != 0):
            convolve_any(conv)
            with nc.Fori(0, 1) as once:
                with nc.Block() as block:
                    @block.vector
                    def _(dve):
                        step = Chain(dve, s_v)
                        step(dve.tensor_tensor(conv[:, :, :], conv[:, :, :], z_sb[:, :, :], ALU.add))
                        step(dve.tensor_tensor(conv[:, :, :], conv[:, :, :], wide(dinv[:, :], HID), ALU.mult))
                clear([s_v])
            with nc.Fori(0, NB) as i:
                tiles = bass.ds(i * BT, BT)
                with nc.Block() as block:
                    @block.vector
                    def _(dve):
                        dve.tensor_copy(bt0[:, :, 0:HID], conv[:, tiles, :]).then_inc(s_res, 1)
                        dve.wait_ge(s_mm, 1)
                        step = Chain(dve, s_v)
                        add_banks(dve, step, bt2, 2, 3, b2_sb)
                        step(dve.tensor_tensor(x_sb[:, tiles, :], x_sb[:, tiles, :], bt2[:, :, :], ALU.add))

                    @block.tensor
                    def _(pe):
                        pe.wait_ge(s_res, 1)
                        for t, place in enumerate(halves(0, 1, BT)):
                            last = pe.transpose(place[0:HID, :], bt0[:, t, 0:HID], ident[:, :])
                        last.then_inc(s_tr, 1)
                        pe.wait_ge(s_ev, 1)
                        for t, place in enumerate(halves(2, 3, BT)):
                            last = pe.matmul(place, bt1[0:HID, t, :], w2_sb[:, :], start=True, stop=True)
                        last.then_inc(s_mm, 1)

                    @block.scalar
                    def _(act):
                        act.wait_ge(s_tr, 1)
                        act.copy(bt1[0:HID, 0:GT, :], block_of(0, GT)[0:HID])
                        act.copy(bt1[0:HID, GT:BT, :], block_of(1, BT - GT)[0:HID]).then_inc(s_ev, 1)
                clear(dense_sems)
            with nc.Fori(0, 1) as once:
                with nc.Block() as block:
                    @block.sync
                    def _(sp):
                        sp.dma_start(out[0:FULL * P, :].rearrange("(t p) f -> p t f", p=P), x_sb[:, 0:FULL, :])\
                          .then_inc(s_st, 16)
                        sp.dma_start(out[FULL * P:N, :], x_sb[0:TAIL, FULL, :]).then_inc(s_st, 16)
                        sp.wait_ge(s_st, 32)


_INS = ["x", "src", "dst", "edge_attr_128", "L0_gnn_W_msg", "L0_gnn_b_msg", "L0_gnn_W_upd", "L0_gnn_b_upd",
        "L0_gnn_gamma", "L0_gnn_beta", "L1_gnn_W1", "L1_gnn_b1", "L1_gnn_W2", "L1_gnn_b2"]


def kernel(**inputs):
    import numpy as _np
    import concourse.bacc as _bacc
    from concourse import mybir as _mybir
    from concourse.bass_utils import run_bass_kernel_spmd as _run

    nc = _bacc.Bacc("TRN2", target_bir_lowering=False, num_devices=1)
    arrays, args = {}, []
    for name in _INS:
        a = _np.ascontiguousarray(inputs[name])
        arrays[f"in_{name}"] = a
        args.append(nc.dram_tensor(f"in_{name}", a.shape, _mybir.dt.from_np(a.dtype), kind="ExternalInput").ap())
    args.append(nc.dram_tensor("out_nodes", arrays["in_x"].shape, _mybir.dt.float32, kind="ExternalOutput").ap())
    gnn_kernel(nc, *args)
    r = _run(nc, [arrays], core_ids=[0])
    return r.results[0]["out_nodes"]
```
